# Optimizing a Trainium2 kernel written in Bass

```python
import numpy as np
import jax
import jax.numpy as jnp

def _softmax(x, axis=-1):
    return jax.nn.softmax(x, axis=axis)

def _gelu(x):
    return jax.nn.gelu(x, approximate=True)

def _silu(x):
    return jax.nn.silu(x)

def _sigmoid(x):
    return jax.nn.sigmoid(x)

def _layernorm(x, axis=-1, eps=1e-05):
    m = jnp.mean(x, axis=axis, keepdims=True)
    v = jnp.var(x, axis=axis, keepdims=True)
    return (x - m) / jnp.sqrt(v + eps)

def _scatter_add(tgt, idx, src, axis=0):
    return tgt.at[idx].add(src)

def _segment_sum(src, seg, n):
    return jax.ops.segment_sum(src, seg, n)
kernel_name = 'mk_vit_tower_cls_d1_tok_img1024_r4_246f59'

def setup_inputs(seed: int=0):
    np.random.seed(seed)
    _w = jnp.asarray

    def _rec_inputs():
        import jax
        import jax.numpy as jnp
        _rk = jax.random.key(seed)
        x = -0.000222058 + 0.999998 * jax.random.normal(jax.random.fold_in(_rk, 1), (32, 128, 128, 3), jnp.float32)
        cls_tok = 0.02 * jax.random.normal(jax.random.fold_in(_rk, 5), (1, 1, 256), jnp.float32)
        return (x, cls_tok)
    x, cls_tok = _rec_inputs()

    def _L0_tok_setup():
        import jax, jax.numpy as jnp
        import numpy as np
        PATCH = 16
        CHANNELS = 3
        HIDDEN = 256
        key = jax.random.key(seed)
        k1, k2 = jax.random.split(key)
        inputs = jax.random.normal(k1, (32, 128, 128, 3), dtype=jnp.float32)
        fan_in = CHANNELS * PATCH * PATCH
        W = jax.random.normal(k2, (fan_in, HIDDEN), dtype=jnp.float32) / np.sqrt(fan_in)
        return {'inputs': inputs, 'W': W}
    _L0_tok_all = _L0_tok_setup()
    _L0_tok_in = {k: v for k, v in _L0_tok_all.items() if k in ('W',)}
    del _L0_tok_all

    def _L0_attn_setup():
        import math
        import jax, jax.numpy as jnp
        import numpy as np
        EMBED_DIM = 256
        NUM_HEADS = 16
        FACTOR = 5
        key = jax.random.key(seed)
        kx, kw, kb, kow, kob = jax.random.split(key, 5)
        B, S, E = (8, 1024, EMBED_DIM)
        scale = 1.0 / math.sqrt(E)
        x = jax.random.normal(kx, (B, S, E), dtype=jnp.float32)
        in_proj_w = jax.random.uniform(kw, (3 * E, E), dtype=jnp.float32, minval=-scale, maxval=scale)
        in_proj_b = jnp.zeros((3 * E,), dtype=jnp.float32)
        out_w = jax.random.uniform(kow, (E, E), dtype=jnp.float32, minval=-scale, maxval=scale)
        out_b = jnp.zeros((E,), dtype=jnp.float32)
        return {'x': x, 'in_proj_w': in_proj_w, 'in_proj_b': in_proj_b, 'out_w': out_w, 'out_b': out_b}
    _L0_attn_all = _L0_attn_setup()
    _L0_attn_in = {k: v for k, v in _L0_attn_all.items() if k in ('in_proj_w', 'in_proj_b', 'out_w', 'out_b')}
    del _L0_attn_all

    def _L0_ffn_setup():
        import jax, jax.numpy as jnp
        import numpy as np
        BLOCK = 16
        _GRID = jnp.array([0.0, 0.5, 1.0, 1.5, 2.0, 3.0, 4.0, 6.0], dtype=jnp.float32)
        _MID = jnp.array([0.25, 0.75, 1.25, 1.75, 2.5, 3.5, 5.0], dtype=jnp.float32)

        def fp4_quant_dequant(x):
            shape = x.shape
            xb = x.reshape(shape[:-1] + (shape[-1] // BLOCK, BLOCK))
            scale = jnp.max(jnp.abs(xb), axis=-1, keepdims=True) / 6.0
            scale = jnp.maximum(scale, jnp.float32(1e-12))
            xn = xb / scale
            idx = jnp.searchsorted(_MID, jnp.abs(xn))
            q = _GRID[idx] * jnp.sign(xn) * scale
            return q.reshape(shape)

        def fp4_linear(x, w):
            xq = fp4_quant_dequant(x)
            wq = fp4_quant_dequant(w)
            return jnp.einsum('bsk,nk->bsn', xq, wq)
        key = jax.random.key(seed)
        k1, k2, k3, k4 = jax.random.split(key, 4)
        H, I = (256, 704)
        x = jax.random.normal(k1, (4, 1024, H), dtype=jnp.float32)
        w_gate = jax.random.normal(k2, (I, H), dtype=jnp.float32) * 0.02
        w_up = jax.random.normal(k3, (I, H), dtype=jnp.float32) * 0.02
        w_down = jax.random.normal(k4, (H, I), dtype=jnp.float32) * 0.02
        return {'x': x, 'w_gate': w_gate, 'w_up': w_up, 'w_down': w_down}
    _L0_ffn_all = _L0_ffn_setup()
    _L0_ffn_in = {k: v for k, v in _L0_ffn_all.items() if k in ('w_gate', 'w_up', 'w_down')}
    del _L0_ffn_all
    return {'x': x, 'cls_tok': cls_tok, 'L0_tok_W': _L0_tok_in['W'], 'L0_attn_in_proj_w': _L0_attn_in['in_proj_w'], 'L0_attn_in_proj_b': _L0_attn_in['in_proj_b'], 'L0_attn_out_w': _L0_attn_in['out_w'], 'L0_attn_out_b': _L0_attn_in['out_b'], 'L0_ffn_w_gate': _L0_ffn_in['w_gate'], 'L0_ffn_w_up': _L0_ffn_in['w_up'], 'L0_ffn_w_down': _L0_ffn_in['w_down']}

def reference(x, cls_tok, L0_tok_W, L0_attn_in_proj_w, L0_attn_in_proj_b, L0_attn_out_w, L0_attn_out_b, L0_ffn_w_gate, L0_ffn_w_up, L0_ffn_w_down):
    import jax
    import jax.numpy as jnp

    def _L0_tok_ref(inputs, W):
        import jax, jax.numpy as jnp
        import numpy as np
        PATCH = 16
        CHANNELS = 3
        HIDDEN = 256
        if inputs.shape[1] == CHANNELS and inputs.shape[-1] != CHANNELS:
            inputs = jnp.transpose(inputs, (0, 2, 3, 1))
        b, h, w, c = inputs.shape
        p = PATCH
        patches = inputs.reshape(b, h // p, p, w // p, p, c)
        patches = jnp.transpose(patches, (0, 1, 3, 2, 4, 5))
        patches = patches.reshape(b, -1, p * p * c)
        return jnp.einsum('bnf,fh->bnh', patches, W)

    def _L0_attn_ref(x, in_proj_w, in_proj_b, out_w, out_b):
        import math
        import jax, jax.numpy as jnp
        import numpy as np
        EMBED_DIM = 256
        NUM_HEADS = 16
        FACTOR = 5
        B, S, E = x.shape
        H = NUM_HEADS
        hd = E // H
        k = max(1, int(FACTOR * math.log(S + 1)))
        k = min(k, S)
        energy = jnp.linalg.norm(x, axis=-1)
        _, topk_idx = jax.lax.top_k(energy, k)
        q_tok = jnp.take_along_axis(x, topk_idx[..., None], axis=1)
        Wq, Wk, Wv = jnp.split(in_proj_w, 3, axis=0)
        bq, bk, bv = jnp.split(in_proj_b, 3, axis=0)
        q = (q_tok @ Wq.T + bq).reshape(B, k, H, hd)
        kk = (x @ Wk.T + bk).reshape(B, S, H, hd)
        v = (x @ Wv.T + bv).reshape(B, S, H, hd)
        scores = jnp.einsum('bqhd,bshd->bhqs', q, kk) / math.sqrt(hd)
        attn = jax.nn.softmax(scores, axis=-1)
        ctx = jnp.einsum('bhqs,bshd->bqhd', attn, v).reshape(B, k, E)
        out_sel = ctx @ out_w.T + out_b
        default = jnp.mean(x, axis=1)
        result = jnp.broadcast_to(default[:, None, :], (B, S, E))
        batch_ar = jnp.arange(B)[:, None]
        result = result.at[batch_ar, topk_idx].set(out_sel)
        return result

    def _L0_ffn_ref(x, w_gate, w_up, w_down):
        import jax, jax.numpy as jnp
        import numpy as np
        BLOCK = 16
        _GRID = jnp.array([0.0, 0.5, 1.0, 1.5, 2.0, 3.0, 4.0, 6.0], dtype=jnp.float32)
        _MID = jnp.array([0.25, 0.75, 1.25, 1.75, 2.5, 3.5, 5.0], dtype=jnp.float32)

        def fp4_quant_dequant(x):
            shape = x.shape
            xb = x.reshape(shape[:-1] + (shape[-1] // BLOCK, BLOCK))
            scale = jnp.max(jnp.abs(xb), axis=-1, keepdims=True) / 6.0
            scale = jnp.maximum(scale, jnp.float32(1e-12))
            xn = xb / scale
            idx = jnp.searchsorted(_MID, jnp.abs(xn))
            q = _GRID[idx] * jnp.sign(xn) * scale
            return q.reshape(shape)

        def fp4_linear(x, w):
            xq = fp4_quant_dequant(x)
            wq = fp4_quant_dequant(w)
            return jnp.einsum('bsk,nk->bsn', xq, wq)
        gate = fp4_linear(x, w_gate)
        y = fp4_linear(x, w_up)
        h = jax.nn.silu(gate) * y
        return fp4_linear(h, w_down)
    h = _L0_tok_ref(x, L0_tok_W)
    h = jnp.concatenate([jnp.broadcast_to(cls_tok, (h.shape[0], 1, h.shape[2])), h], axis=1)
    h = h + _L0_attn_ref(_layernorm(h, axis=-1), L0_attn_in_proj_w, L0_attn_in_proj_b, L0_attn_out_w, L0_attn_out_b)
    h = h + _L0_ffn_ref(_layernorm(h, axis=-1), L0_ffn_w_gate, L0_ffn_w_up, L0_ffn_w_down)
    return h

_drawn_inputs = setup_inputs


def setup_inputs(seed=0):
    import zlib

    import numpy as np

    out = dict(_drawn_inputs(seed))
    spreads = {'L0_attn_in_proj_b': (0.0, 0.1), 'L0_attn_out_b': (0.0, 0.1)}
    factors = {'cls_tok': 12.785}
    for name, (base, spread) in spreads.items():
        noise = np.random.default_rng([zlib.crc32(name.encode()), seed]).standard_normal(out[name].shape)
        drawn = base * np.exp(spread * noise) if base else spread * noise
        out[name] = jnp.asarray(drawn.astype(out[name].dtype))
    for name, factor in factors.items():
        out[name] = (out[name] * factor).astype(out[name].dtype)
    return out
```

```python
from contextlib import ExitStack

import concourse.bass as bass
from concourse import mybir

ALU = mybir.AluOpType
ACT = mybir.ActivationFunctionType
F32 = mybir.dt.float32
F32R = mybir.dt.float32r
U32 = mybir.dt.uint32
X = mybir.AxisListType.X

P = 128
B = 32
D = 256
T = 65
NP_TOK = T - 1
F = 768
TILES = B * NP_TOK // P
KG = 32
KIND = P // KG
BLOCKS = (512, 256)
UNROLL = 4
QUADS = 4
QW = TILES // QUADS * D
QT = TILES // QUADS
HEADS = 16
HD = D // HEADS
TOPK = 20
I = 704
IC = [(c, min(P, I - c)) for c in range(0, I, P)]
FB = 16
GRID_STEPS = [(0.25, 0.5), (0.75, 0.5), (1.25, 0.5), (1.75, 0.5), (2.5, 1.0), (3.5, 1.0), (5.0, 2.0)]
HI = 0xFFFFF000
EPS = 1e-5


def build_vit(nc, xT, cls_tok, w_tok, in_wT, in_b, in_bT, out_wT, out_b, w_gate, w_up, w_down,
              feature_masks, earlier, head_mask, identity, out):
    with ExitStack() as ctx:
        def sb(name, shape, dt=F32):
            return ctx.enter_context(nc.sbuf_tensor(name, shape, dt))

        def sem(name):
            return ctx.enter_context(nc.semaphore(name))

        W8 = B * D
        work = sb("work", [P, 4 * W8])
        psum = ctx.enter_context(nc.psum_tensor("psum", [P, 8, 512], F32))
        ident = sb("ident", [P, P])
        weights = sb("weights", [P, 3 * 2 * D + 2 * D + 4 * I + len(IC) * D])

        def quads(at):
            return work[:, at:at + QUADS * QW].rearrange("p (q n) -> p q n", q=QUADS)
        total, back, restore, rest, acc, first = (quads(n * QUADS * QW) for n in range(6))
        raw = work[:, 24576:24576 + B * NP_TOK]
        upper = work[:, 26624:26624 + B * NP_TOK]
        tok_split = sb("tok_split", [P, B * NP_TOK], F32R)
        NG = F // KG
        wsplit = weights[:, 0:NG * D].rearrange("p (g n) -> p g n", g=NG)
        wraw = work[:, 0:NG * D].rearrange("p (g n) -> p g n", g=NG)
        wup = work[:, W8:W8 + NG * D].rearrange("p (g n) -> p g n", g=NG)
        wrow = sb("wrow", [P, 2, 2 * D], F32R)
        masks = sb("masks", [P, 2, KG])

        def rows(k):
            return work[0:T, k * W8:(k + 1) * W8].rearrange("p (b n) -> p b n", b=B)
        H, XN, T1, T2 = rows(0), rows(1), rows(2), rows(3)

        small = sb("small", [P, 18, B])
        sm = lambda k: small[0:T, k, :]
        lanes = sb("lanes", [P, B * 16])
        wq = weights[:, 0:1536].rearrange("p (a n) -> p a n", a=2)
        wo = weights[:, 1536:2048].rearrange("p (a n) -> p a n", a=2)
        wgu = weights[:, 2048:2048 + 4 * I].rearrange("p (w a n) -> p w a n", w=2, a=2)
        wd = weights[:, 2048 + 4 * I:].rearrange("p (c n) -> p c n", c=len(IC))
        in_bias = sb("in_bias", [P, 6])
        row_bias = sb("row_bias", [1, 2, D])
        ones = sb("ones", [P, T])
        hmask = sb("hmask", [P, 8])

        sems = {}
        def S(name):
            if name not in sems:
                sems[name] = sem(name)
            return sems[name]

        GROUPS = [n // KG for n in BLOCKS]
        PER_GROUP = KG // UNROLL
        NSTEP = UNROLL * QUADS

        at = [3 * W8]
        def scratch(parts, *shape):
            n = 1
            for x in shape:
                n *= x
            v = work[0:parts, at[0]:at[0] + n]
            at[0] += n
            if len(shape) == 2:
                v = v.rearrange("p (a b) -> p a b", a=shape[0])
            if len(shape) == 3:
                v = v.rearrange("p (a b c) -> p a b c", a=shape[0], b=shape[1])
            return v
        xb = scratch(T, D)
        xbT = scratch(P, 2, T)
        qT = scratch(P, 2, T)
        kT = scratch(P, 2, T)
        kM = scratch(P, 2, 8, T)
        vS = scratch(T, D)
        sc = scratch(T, HEADS, T)
        pT = scratch(T, HEADS, T)
        cn = scratch(T, D)
        cT = scratch(P, 2, T)
        mx = scratch(T, HEADS)
        den = scratch(T, HEADS)
        rden = scratch(T, HEADS)
        assert at[0] <= 4 * W8
        at[0] = 3 * W8 + D + 2 * T
        gate = scratch(T, I)
        hid = scratch(T, I)
        qa, qc, qd, qe = (scratch(T, I) for _ in range(4))
        hT = scratch(P, len(IC), T)
        bmax = scratch(T, 2, I // FB)
        assert at[0] <= 4 * W8
        at[0] = 2 * W8
        wld, wa, wc, wdd, we = (scratch(P, 1536) for _ in range(5))
        wmax = scratch(P, 2, 96)
        at[0] = 2 * W8
        earl, gt, eq = (scratch(B, T, T) for _ in range(3))
        tokE = sb("tokE", [B, 3, T])

        block = ctx.enter_context(nc.Block())

        @block.sync
        def _(sp):
            for j in range(KIND):
                sp.dma_start(wraw[KG * j:KG * (j + 1), :, :],
                             w_tok.rearrange("(g k) n -> k g n", k=KG)).then_inc(S("w_dma"), 16)
            sp.dma_start(masks[:, :, :], feature_masks).then_inc(S("const_dma"), 16)
            sp.dma_start(ident[:, :], identity).then_inc(S("const_dma"), 16)
            sp.dma_start(hmask[:, :], head_mask).then_inc(S("const_dma"), 16)
            sp.dma_start(in_bias[:, :], in_bT).then_inc(S("const_dma"), 16)
            sp.dma_start(row_bias[:, 0, :], in_b[2 * D:3 * D].rearrange("(a n) -> a n", a=1)).then_inc(S("const_dma"), 16)
            sp.dma_start(row_bias[:, 1, :], out_b.rearrange("(a n) -> a n", a=1)).then_inc(S("const_dma"), 16)
            g0 = 0
            for n in GROUPS:
                with sp.Fori(0, n) as g:
                    sp.wait_ge(S("raw_free"), g + (g0 + 1))
                    for j in range(KIND):
                        sp.dma_start(raw[KG * j:KG * (j + 1), :],
                                     xT[bass.ds((g + g0) * KG, KG), :]).then_inc(S("raw_dma"), 16)
                g0 += n
            sp.wait_ge(S("tokens_done"), 1)
            t = acc.rearrange("p q (t n) -> p (q t) n", n=D)
            for half in range(2):
                sp.dma_start(H[0:NP_TOK, half:B:2, :],
                             t[NP_TOK * half:NP_TOK * (half + 1), :, :]).then_inc(S("h_dma"), 16)
            sp.dma_start(H[NP_TOK:T, :, :], cls_tok[0].unsqueeze(1).to_broadcast([1, B, D])).then_inc(S("h_dma"), 16)
            sp.dma_start(wq[:, :, :], in_wT.rearrange("(a p) n -> p a n", p=P)).then_inc(S("h_dma"), 16)
            sp.dma_start(wo[:, :, :], out_wT.rearrange("(a p) n -> p a n", p=P)).then_inc(S("h_dma"), 16)
            for w, src in enumerate((w_gate, w_up, w_down)):
                sp.wait_ge(S("wld_free"), w + 1)
                if w < 2:
                    d3 = wld.rearrange("p (c n) -> p c n", c=len(IC))
                    sp.dma_start(d3[:, 0:5, :], src[0:5 * P, :].rearrange("(c p) n -> p c n", p=P)).then_inc(S("wld_dma"), 16)
                    sp.dma_start(d3[0:I - 5 * P, 5, :], src[5 * P:I, :]).then_inc(S("wld_dma"), 16)
                else:
                    sp.dma_start(wld[:, 0:2 * I].rearrange("p (a n) -> p a n", a=2),
                                 src.rearrange("(a p) n -> p a n", p=P)).then_inc(S("wld_dma"), 32)
            sp.wait_ge(S("lanes_free"), 1)
            sp.dma_start(earl[:, :, :], earlier).then_inc(S("earl_dma"), 16)
            sp.wait_ge(S("f_start"), B + 1)
            o = out.rearrange("b t n -> t b n")
            sp.dma_start(o[0:1, :, :], H[NP_TOK:T, :, :]).then_inc(S("out_dma"), 16)
            sp.dma_start(o[1:T, :, :], H[0:NP_TOK, :, :]).then_inc(S("out_dma"), 16)
            sp.wait_ge(S("out_dma"), 32)

        def attention_act(act):
            with act.Fori(0, B) as b:
                act.wait_ge(S("a_start"), b + 1)
                act.activation(xb, XN[:, bass.ds(b, 1), :].rearrange("p a n -> p (a n)"), ACT.Copy).then_inc(S("a_x"), 1)
                act.wait_ge(S("a_qkv"), b + 1)
                for o in range(2):
                    act.activation(qT[:, o, :], psum[:, 1, o * T:(o + 1) * T], ACT.Identity, bias=in_bias[:, o:o + 1])
                    act.activation(kT[:, o, :], psum[:, 1, (2 + o) * T:(3 + o) * T], ACT.Identity,
                                   bias=in_bias[:, 2 + o:3 + o])
                act.activation(vS, psum[0:T, 2, 0:D], ACT.Copy).then_inc(S("a_kv"), 1)
                act.wait_ge(S("a_sub"), b + 1)
                act.activation(sc, sc, ACT.Exp, scale=float(HD) ** -0.5).then_inc(S("a_exp"), 1)
                act.wait_ge(S("a_pt"), b + 1)
                act.activation(pT.rearrange("p (g h) t -> p g (h t)", g=4), psum[0:T, 3:7, 0:4 * T],
                               ACT.Copy).then_inc(S("a_ptc"), 1)

        def ffn_act(act):
            with act.Fori(0, B) as b:
                act.wait_ge(S("f_start"), b + 1)
                act.activation(xb, XN[:, bass.ds(b, 1), :].rearrange("p a n -> p (a n)"), ACT.Copy).then_inc(S("f_x"), 1)
                act.wait_ge(S("f_gu"), b + 1)
                act.activation(gate.rearrange("p (a n) -> p a n", a=2), psum[0:T, 1:3, 0:I // 2],
                               ACT.Exp, scale=-1.0).then_inc(S("f_e"), 1)
                act.wait_ge(S("f_ht"), b + 1)
                act.activation(hT[:, 0:5, :], psum[:, 5, 0:5 * T].rearrange("p (c t) -> p c t", c=5), ACT.Copy)
                act.activation(hT[0:I - 5 * P, 5, :], psum[0:I - 5 * P, 5, 5 * T:6 * T], ACT.Copy).then_inc(S("f_htc"), 1)

        @block.scalar
        def _(act):
            g0 = 0
            act.wait_ge(S("w_split"), 4)
            act.wait_ge(S("const_dma"), 96)
            for n in GROUPS:
                with act.Fori(0, n) as g:
                    act.wait_ge(S("split_hi"), g + (g0 + 1))
                    act.activation(tok_split[0:2 * KG, :], upper[0:2 * KG, :], ACT.Copy).then_inc(S("split_act"), 1)
                    with act.Fori(0, PER_GROUP) as c:
                        for u in range(UNROLL):
                            act.wait_ge(S("products"), (((g + g0) * PER_GROUP + c) * UNROLL + (u + 1)) * QUADS)
                            for part in range(2):
                                ins = act.activation(wrow[:, u % 2, part * D:(part + 1) * D],
                                                     wsplit[:, bass.ds(g + g0, 1), :].rearrange("p a n -> p (a n)"),
                                                     ACT.Copy, scale=masks[:, part, bass.ds(c * UNROLL + u, 1)])
                            ins.then_inc(S("row_ready"), 1)
                g0 += n
            for k in range(3):
                act.wait_ge(S("sqrt_in"), k + 1)
                act.activation(sm(1), sm(0), ACT.Sqrt).then_inc(S("sqrt_out"), 1)
                if k == 1:
                    attention_act(act)
            ffn_act(act)

        @block.gpsimd
        def _(pool):
            def step(i, q):
                pool.wait_ge(S("total_ready"), i + 1)
                pool.tensor_tensor(back[:, q, :], total[:, q, :], acc[:, q, :], ALU.subtract).then_inc(S("back_ready"), 1)
                pool.wait_ge(S("back_ready"), i + 1)
                pool.tensor_tensor(restore[:, q, :], total[:, q, :], back[:, q, :], ALU.subtract).then_inc(S("restore_mid"), 1)
                pool.wait_ge(S("restore_mid"), i + 1)
                pool.tensor_tensor(restore[:, q, :], acc[:, q, :], restore[:, q, :], ALU.subtract).then_inc(S("restore_ready"), 1)
            g0 = 0
            for n in GROUPS:
                with pool.Fori(0, n) as g:
                    with pool.Fori(0, PER_GROUP) as c:
                        for s in range(NSTEP):
                            step(((g + g0) * PER_GROUP + c) * NSTEP + s, s % QUADS)
                g0 += n

        @block.tensor
        def _(pe):
            g0 = 0
            for n in GROUPS:
                with pe.Fori(0, n) as g:
                    with pe.Fori(0, PER_GROUP) as c:
                        for s in range(NSTEP):
                            it = (g + g0) * PER_GROUP + c
                            u, q = s // QUADS, s % QUADS
                            if s == 0:
                                pe.wait_ge(S("split_act"), g + (g0 + 1))
                                pe.wait_ge(S("split_dve"), g + (g0 + 1))
                            if q == 0:
                                pe.wait_ge(S("row_ready"), it * UNROLL + (u + 1))
                            pe.wait_ge(S("products_used"), it * NSTEP + (s + 1))
                            for t in range(QT):
                                last = pe.matmul(psum[:, (s % 2) * QT + t, :],
                                                 tok_split[:, (q * QT + t) * P:(q * QT + t + 1) * P],
                                                 wrow[:, u % 2, :], start=True, stop=True)
                            last.then_inc(S("products"), 1)
                g0 += n
            for w in range(3):
                pe.wait_ge(S("w_quant"), w + 1)
                if w < 2:
                    v = wld.rearrange("p (c n) -> p c n", c=len(IC))
                    for a in range(2):
                        for c, (_, m) in enumerate(IC):
                            last = pe.transpose(psum[:, a * 2 + c // 4, (c % 4) * P:(c % 4) * P + m],
                                                v[0:m, c, a * P:(a + 1) * P], ident[0:m, 0:m])
                else:
                    v = wld[:, 0:2 * I].rearrange("p (a n) -> p a n", a=2)
                    for c, (o, m) in enumerate(IC):
                        for a in range(2):
                            last = pe.transpose(psum[0:m, c // 2, (c % 2) * D + a * P:(c % 2) * D + (a + 1) * P],
                                                v[:, a, o:o + m], ident[:, :])
                last.then_inc(S("w_turned"), 1)
            pe.wait_ge(S("energy"), 1)
            pe.transpose(psum[0:B, 0, 0:T], sm(4), ident[0:T, 0:T]).then_inc(S("energy_t"), 1)
            pe.wait_ge(S("picked"), 1)
            pe.transpose(psum[0:T, 1, 0:B], tokE[:, 2, :], ident[0:B, 0:B]).then_inc(S("picked_t"), 1)
            for r in range(2):
                pe.wait_ge(S("banks_read"), r + 1)
                for n in range(8):
                    last = pe.matmul(psum[0:T, n, :], ones[0:T, :],
                                     XN.rearrange("p b n -> p (b n)")[:, (8 * r + n) * 512:(8 * r + n + 1) * 512],
                                     start=True, stop=True)
                last.then_inc(S("mean_sum"), 1)
            with pe.Fori(0, B) as b:
                pe.wait_ge(S("a_x"), b + 1)
                for a in range(2):
                    last = pe.transpose(psum[:, 0, a * T:(a + 1) * T], xb[:, a * P:(a + 1) * P], ident[0:T, 0:T])
                last.then_inc(S("a_xt"), 1)
                pe.wait_ge(S("a_xtc"), b + 1)
                for o in range(4):
                    for a in range(2):
                        pe.matmul(psum[:, 1, o * T:(o + 1) * T], wq[:, a, o * P:(o + 1) * P], xbT[:, a, :],
                                  start=(a == 0), stop=(a == 1))
                for a in range(2):
                    pe.matmul(psum[0:T, 2, 0:D], xbT[:, a, :], wq[:, a, 2 * D:3 * D], start=(a == 0), stop=False)
                pe.matmul(psum[0:T, 2, 0:D], ones[0:1, :], row_bias[:, 0, :], start=False, stop=True).then_inc(S("a_qkv"), 1)
                pe.wait_ge(S("a_km"), b + 1)
                for g in range(4):
                    last = pe.matmul(psum[0:T, 3 + g, 0:4 * T], qT[:, g // 2, :],
                                     kM[:, g // 2, (g % 2) * 4:(g % 2) * 4 + 4, :].rearrange("p h t -> p (h t)"),
                                     start=True, stop=True)
                last.then_inc(S("a_sc"), 1)
                pe.wait_ge(S("a_exp"), b + 1)
                for h in range(HEADS):
                    last = pe.transpose(psum[0:T, 3 + h // 4, (h % 4) * T:(h % 4 + 1) * T], sc[:, h, :], ident[0:T, 0:T])
                last.then_inc(S("a_pt"), 1)
                pe.wait_ge(S("a_ptc"), b + 1)
                for h in range(HEADS):
                    last = pe.matmul(psum[0:T, 7, h * HD:(h + 1) * HD], pT[:, h, :], vS[:, h * HD:(h + 1) * HD],
                                     start=True, stop=True)
                last.then_inc(S("a_pv"), 1)
                pe.wait_ge(S("a_cn"), b + 1)
                for a in range(2):
                    last = pe.transpose(psum[:, 0, a * T:(a + 1) * T], cn[:, a * P:(a + 1) * P], ident[0:T, 0:T])
                last.then_inc(S("a_ct"), 1)
                pe.wait_ge(S("a_ctc"), b + 1)
                for a in range(2):
                    pe.matmul(psum[0:T, 1, 0:D], cT[:, a, :], wo[:, a, :], start=(a == 0), stop=False)
                pe.matmul(psum[0:T, 1, 0:D], ones[0:1, :], row_bias[:, 1, :], start=False, stop=True).then_inc(S("a_o"), 1)
            with pe.Fori(0, B) as b:
                pe.wait_ge(S("f_x"), b + 1)
                for a in range(2):
                    last = pe.transpose(psum[:, 0, a * T:(a + 1) * T], xb[:, a * P:(a + 1) * P], ident[0:T, 0:T])
                last.then_inc(S("f_xt"), 1)
                pe.wait_ge(S("f_xtc"), b + 1)
                for w in range(2):
                    for n in range(2):
                        for a in range(2):
                            last = pe.matmul(psum[0:T, 1 + 2 * w + n, 0:I // 2], xbT[:, a, :],
                                             wgu[:, w, a, n * (I // 2):(n + 1) * (I // 2)], start=(a == 0), stop=(a == 1))
                last.then_inc(S("f_gu"), 1)
                pe.wait_ge(S("f_q"), b + 1)
                for c, (o, m) in enumerate(IC):
                    last = pe.transpose(psum[0:m, 5, c * T:(c + 1) * T], hid[:, o:o + m], ident[0:T, 0:T])
                last.then_inc(S("f_ht"), 1)
                pe.wait_ge(S("f_htc"), b + 1)
                for c, (_, m) in enumerate(IC):
                    last = pe.matmul(psum[0:T, 6, 0:D], hT[0:m, c, :], wd[0:m, c, :], start=(c == 0), stop=(c == len(IC) - 1))
                last.then_inc(S("f_o"), 1)

        @block.vector
        def _(dve):
            count = [0]

            def link(ins):
                count[0] += 1
                ins.then_inc(S("vec"), 1)
                dve.wait_ge(S("vec"), count[0])

            dve.sem_inc(S("raw_free"), 1)
            dve.sem_inc(S("products"), 2 * QUADS)
            dve.sem_inc(S("products_used"), 2)
            dve.wait_ge(S("w_dma"), 64)
            link(dve.tensor_scalar(wup.bitcast(U32), wraw.bitcast(U32), HI, None, ALU.bitwise_and))
            for j in range(KIND):
                r = slice(KG * j, KG * (j + 1))
                if j % 2 == 0:
                    dve.tensor_copy(wsplit[r], wup[r]).then_inc(S("w_split"), 1)
                else:
                    dve.tensor_tensor(wsplit[r], wraw[r], wup[r], ALU.subtract).then_inc(S("w_split"), 1)
            dve.wait_ge(S("w_split"), 4)

            def bank(i, part):
                s = (i % 2) * QT
                return psum[:, s:s + QT, part * D:(part + 1) * D]

            def q3(v, q):
                return v[:, q, :].rearrange("p (t n) -> p t n", n=D)

            def add_upper(i, s, blk):
                dve.wait_ge(S("products"), i + (1 + 2 * QUADS))
                dve.wait_ge(S("acc_ready"), i + (1 + 4 * blk))
                dve.tensor_tensor(q3(total, s % QUADS), bank(s, 0), q3(acc, s % QUADS), ALU.add).then_inc(S("total_ready"), 1)

            def rest_upper(i, s):
                dve.wait_ge(S("back_ready"), i + 1)
                dve.tensor_tensor(q3(rest, s % QUADS), bank(s, 0), q3(back, s % QUADS), ALU.subtract).then_inc(S("rest_a"), 1)

            def rest_lower(i, s):
                dve.wait_ge(S("rest_a"), i + 1)
                dve.tensor_tensor(q3(rest, s % QUADS), bank(s, 1), q3(rest, s % QUADS), ALU.add).then_inc(S("products_used"), 1)

            def rest_all(i, s):
                dve.wait_ge(S("products_used"), i + 3)
                dve.wait_ge(S("restore_ready"), i + 1)
                dve.tensor_tensor(rest[:, s % QUADS, :], rest[:, s % QUADS, :], restore[:, s % QUADS, :],
                                  ALU.add).then_inc(S("rest_c"), 1)

            def add_rest(i, s):
                dve.wait_ge(S("rest_c"), i + 1)
                dve.tensor_tensor(acc[:, s % QUADS, :], total[:, s % QUADS, :], rest[:, s % QUADS, :],
                                  ALU.add).then_inc(S("acc_ready"), 1)

            g0 = 0
            for blk, n in enumerate(GROUPS):
                dve.memset(acc, 0.0).then_inc(S("acc_ready"), 4)
                with dve.Fori(0, n) as g:
                    dve.wait_ge(S("raw_dma"), (g + (g0 + 1)) * 64)
                    dve.tensor_scalar(upper.bitcast(U32), raw.bitcast(U32), HI, None, ALU.bitwise_and).then_inc(S("split_hi"), 1)
                    dve.wait_ge(S("split_hi"), g + (g0 + 1))
                    dve.tensor_tensor(tok_split[2 * KG:P, :], raw[2 * KG:P, :], upper[2 * KG:P, :],
                                      ALU.subtract).then_inc(S("split_dve"), 1)
                    dve.wait_ge(S("split_dve"), g + (g0 + 1))
                    dve.sem_inc(S("raw_free"), 1)
                    with dve.Fori(0, PER_GROUP) as c:
                        for slot in range(NSTEP + 2):
                            base = ((g + g0) * PER_GROUP + c) * NSTEP
                            if slot < NSTEP:
                                add_upper(base + slot, slot, blk)
                            if 1 <= slot <= NSTEP:
                                rest_upper(base + (slot - 1), slot - 1)
                            if slot >= 2:
                                rest_all(base + (slot - 2), slot - 2)
                            if 1 <= slot <= NSTEP:
                                rest_lower(base + (slot - 1), slot - 1)
                            if slot >= 2:
                                add_rest(base + (slot - 2), slot - 2)
                g0 += n
                done = g0 * PER_GROUP * NSTEP + 4 * (blk + 1)
                dve.wait_ge(S("acc_ready"), done)
                if blk == 0:
                    link(dve.tensor_copy(first, acc))
                else:
                    dve.tensor_tensor(acc, first, acc, ALU.add).then_inc(S("tokens_done"), 1)

            def fp4(x, a, c, d, e, top, scale):
                n = x.free_size() // FB
                blocks = lambda v: v.rearrange("p (b s) -> p b s", s=FB)
                wide = lambda v: v.unsqueeze(2).to_broadcast([v.shape[0], n, FB])
                link(dve.tensor_reduce(top, blocks(x), X, ALU.max, apply_absolute_value=True))
                link(dve.tensor_scalar(top, top, 1.0 / 6.0, 1e-12, ALU.mult, ALU.max))
                link(dve.reciprocal(scale, top))
                link(dve.tensor_scalar(a.bitcast(U32), x.bitcast(U32), 0x7FFFFFFF, None, ALU.bitwise_and))
                link(dve.tensor_tensor(blocks(a), blocks(a), wide(scale), ALU.mult))
                link(dve.tensor_scalar(c, a, GRID_STEPS[0][0], None, ALU.is_gt))
                for mid, _ in GRID_STEPS[1:4]:
                    link(dve.scalar_tensor_tensor(out=c, in0=a, scalar=mid, in1=c, op0=ALU.is_gt, op1=ALU.add))
                link(dve.tensor_scalar(d, a, GRID_STEPS[4][0], None, ALU.is_gt))
                link(dve.scalar_tensor_tensor(out=d, in0=a, scalar=GRID_STEPS[5][0], in1=d, op0=ALU.is_gt, op1=ALU.add))
                link(dve.tensor_scalar(e, a, GRID_STEPS[6][0], 2.0, ALU.is_gt, ALU.mult))
                link(dve.tensor_tensor(d, d, e, ALU.add))
                link(dve.scalar_tensor_tensor(out=c, in0=c, scalar=0.5, in1=d, op0=ALU.mult, op1=ALU.add))
                link(dve.tensor_tensor(blocks(c), blocks(c), wide(top), ALU.mult))
                return dve.scalar_tensor_tensor(out=x.bitcast(U32), in0=x.bitcast(U32), scalar=0x80000000,
                                                in1=c.bitcast(U32), op0=ALU.bitwise_and, op1=ALU.bitwise_or)

            dve.wait_ge(S("tokens_done"), 1)
            dve.wait_ge(S("h_dma"), 80)
            dve.memset(ones[:, :], 1.0)
            link(dve.memset(wld, 0.0))
            dve.sem_inc(S("wld_free"), 1)
            for w in range(3):
                dve.wait_ge(S("wld_dma"), 32 * (w + 1))
                n = 6 * D if w < 2 else 2 * I
                fp4(wld[:, 0:n], wa[:, 0:n], wc[:, 0:n], wdd[:, 0:n], we[:, 0:n],
                    wmax[:, 0, 0:n // FB], wmax[:, 1, 0:n // FB]).then_inc(S("w_quant"), 1)
                dve.wait_ge(S("w_turned"), w + 1)
                if w < 2:
                    for a in range(2):
                        dve.tensor_copy(wgu[:, w, a, 0:512], psum[:, a * 2, :])
                        last = dve.tensor_copy(wgu[:, w, a, 512:I], psum[:, a * 2 + 1, 0:I - 512])
                else:
                    for c, (_, m) in enumerate(IC):
                        last = dve.tensor_copy(wd[0:m, c, :], psum[0:m, c // 2, (c % 2) * D:(c % 2 + 1) * D])
                link(last)
                dve.sem_inc(S("wld_free"), 1)

            def wide(v, n=D):
                return v.unsqueeze(2).to_broadcast([T, v.shape[1], n])

            def root(k, n):
                y, yh, yl, r, t = sm(1), sm(13), sm(14), sm(15), sm(16)
                dve.sem_inc(S("sqrt_in"), 1)
                dve.wait_ge(S("sqrt_out"), n)
                link(dve.tensor_scalar(yh.bitcast(U32), y.bitcast(U32), HI, None, ALU.bitwise_and))
                link(dve.tensor_tensor(yl, y, yh, ALU.subtract))
                link(dve.tensor_tensor(t, yh, yh, ALU.mult))
                link(dve.tensor_tensor(r, sm(0), t, ALU.subtract))
                link(dve.scalar_tensor_tensor(out=t, in0=yh, scalar=2.0, in1=yl, op0=ALU.mult, op1=ALU.mult))
                link(dve.tensor_tensor(r, r, t, ALU.subtract))
                link(dve.tensor_tensor(t, yl, yl, ALU.mult))
                link(dve.tensor_tensor(r, r, t, ALU.subtract))
                link(dve.tensor_scalar(t, y, 2.0, 1e-30, ALU.mult, ALU.max))
                link(dve.reciprocal(t, t))
                link(dve.tensor_tensor(r, r, t, ALU.mult))
                link(dve.tensor_tensor(sm(k), y, r, ALU.add))

            def mean_lanes(src, k):
                ln = lanes[0:T, :].rearrange("p (b l) -> p b l", l=16)
                link(dve.tensor_reduce(ln, src.rearrange("p b (i l) -> p b l i", l=16), X, ALU.add))
                link(dve.tensor_tensor(ln[:, :, 0:4], ln[:, :, 0:4], ln[:, :, 4:8], ALU.add))
                link(dve.tensor_tensor(ln[:, :, 8:12], ln[:, :, 8:12], ln[:, :, 12:16], ALU.add))
                link(dve.tensor_tensor(ln[:, :, 0:4], ln[:, :, 0:4], ln[:, :, 8:12], ALU.add))
                link(dve.tensor_tensor(ln[:, :, 0:4:2], ln[:, :, 0:4:2], ln[:, :, 1:4:2], ALU.add))
                link(dve.tensor_tensor(ln[:, :, 0:1], ln[:, :, 0:1], ln[:, :, 2:3], ALU.add))
                link(dve.tensor_scalar(sm(k), ln[:, :, 0], 1.0 / D, None, ALU.mult))

            def squares(src, k):
                link(dve.tensor_tensor(T1, src, src, ALU.mult))
                w8 = lanes[0:T, 0:8 * B].rearrange("p (b w) -> p b w", w=8)
                link(dve.tensor_reduce(w8, T1.rearrange("p b (w s) -> p b w s", s=32), X, ALU.add))
                link(dve.tensor_reduce(sm(k), w8, X, ALU.add))

            def deviation(n):
                mean_lanes(H, 2)
                link(dve.tensor_tensor(XN, H, wide(sm(2)), ALU.subtract))
                squares(XN, 3)
                link(dve.tensor_scalar(sm(0), sm(3), 1.0 / D, EPS, ALU.mult, ALU.add))
                root(5, n)

            deviation(1)
            sh, sl, rs = sm(6), sm(7), sm(8)
            link(dve.tensor_scalar(sh.bitcast(U32), sm(5).bitcast(U32), HI, None, ALU.bitwise_and))
            link(dve.tensor_tensor(sl, sm(5), sh, ALU.subtract))
            link(dve.reciprocal(rs, sm(5)))
            for c in range(4):
                i = slice(8 * c, 8 * c + 8)
                d = XN[:, i, :]
                q0, qh, ql, pr = T1[:, 0:8, :], T1[:, 8:16, :], T1[:, 16:24, :], T1[:, 24:32, :]
                wsh, wsl, wrs = (wide(v[:, i]) for v in (sh, sl, rs))
                rem = T2[:, 0:8, :]
                link(dve.tensor_tensor(q0, d, wrs, ALU.mult))
                link(dve.tensor_scalar(qh.bitcast(U32), q0.bitcast(U32), HI, None, ALU.bitwise_and))
                link(dve.tensor_tensor(ql, q0, qh, ALU.subtract))
                link(dve.tensor_tensor(pr, qh, wsh, ALU.mult))
                link(dve.tensor_tensor(rem, d, pr, ALU.subtract))
                for qx, sx in ((qh, wsl), (ql, wsh), (ql, wsl)):
                    link(dve.tensor_tensor(pr, qx, sx, ALU.mult))
                    link(dve.tensor_tensor(rem, rem, pr, ALU.subtract))
                link(dve.tensor_tensor(rem, rem, wrs, ALU.mult))
                link(dve.tensor_tensor(d, q0, rem, ALU.add))
            squares(XN, 0)
            root(4, 2)
            dve.sem_inc(S("energy"), 1)
            dve.sem_inc(S("lanes_free"), 1)

            dve.wait_ge(S("energy_t"), 1)
            link(dve.tensor_copy(tokE[:, 0, :], psum[0:B, 0, 0:T]))
            ej = tokE[:, 0, :].unsqueeze(1).to_broadcast([B, T, T])
            ei = tokE[:, 0, :].unsqueeze(2).to_broadcast([B, T, T])
            dve.wait_ge(S("earl_dma"), 16)
            dve.tensor_tensor(gt, ej, ei, ALU.is_gt)
            link(dve.tensor_tensor(eq, ej, ei, ALU.is_equal))
            link(dve.tensor_tensor(eq, eq, earl, ALU.mult))
            link(dve.tensor_tensor(gt, gt, eq, ALU.add))
            link(dve.tensor_reduce(tokE[:, 1, :], gt, X, ALU.add))
            dve.tensor_scalar(tokE[:, 2, :], tokE[:, 1, :], float(TOPK), None, ALU.is_lt).then_inc(S("picked"), 1)
            dve.wait_ge(S("picked_t"), 1)
            link(dve.tensor_copy(sm(9), psum[0:T, 1, 0:B]))
            dve.sem_inc(S("banks_read"), 1)
            link(dve.tensor_scalar(sm(10), sm(9), -1.0 / T, 1.0 / T, ALU.mult, ALU.add))
            for r in range(2):
                dve.wait_ge(S("mean_sum"), r + 1)
                i = slice(16 * r, 16 * r + 16)
                ps = psum[0:T, :, :].rearrange("p k (b n) -> p (k b) n", n=D)
                ins = dve.tensor_tensor(T1[:, i, :], ps, wide(sm(10)[:, i]), ALU.mult)
                link(ins)
                dve.sem_inc(S("banks_read"), 1)
            link(dve.tensor_tensor(H, H, T1, ALU.add))
            dve.sem_inc(S("a_start"), 1)

            with dve.Fori(0, B) as b:
                dve.wait_ge(S("a_xt"), b + 1)
                dve.tensor_copy(xbT.rearrange("p a t -> p (a t)"), psum[:, 0, 0:2 * T]).then_inc(S("a_xtc"), 1)
                dve.wait_ge(S("a_kv"), b + 1)
                for o in range(2):
                    ins = dve.tensor_tensor(kM[:, o, :, :], kT[:, o, :].unsqueeze(1).to_broadcast([P, 8, T]),
                                            hmask[:, :].unsqueeze(2).to_broadcast([P, 8, T]), ALU.mult)
                ins.then_inc(S("a_km"), 1)
                dve.wait_ge(S("a_sc"), b + 1)
                s4 = psum[0:T, 3:7, 0:4 * T].rearrange("p g (h t) -> p g h t", t=T)
                dve.tensor_reduce(mx.rearrange("p (g h) -> p g h", g=4), s4, X, ALU.max).then_inc(S("a_mx"), 1)
                dve.wait_ge(S("a_mx"), b + 1)
                for g in range(4):
                    ins = dve.tensor_tensor(sc[:, 4 * g:4 * g + 4, :], s4[:, g, :, :],
                                            mx[:, 4 * g:4 * g + 4].unsqueeze(2).to_broadcast([T, 4, T]), ALU.subtract)
                ins.then_inc(S("a_sub"), 1)
                dve.wait_ge(S("a_exp"), b + 1)
                dve.tensor_reduce(den, sc, X, ALU.add).then_inc(S("a_den"), 1)
                dve.wait_ge(S("a_den"), b + 1)
                dve.reciprocal(rden, den).then_inc(S("a_rden"), 1)
                dve.wait_ge(S("a_pv"), b + 1)
                dve.wait_ge(S("a_rden"), b + 1)
                dve.tensor_tensor(cn.rearrange("p (h e) -> p h e", e=HD), psum[0:T, 7, 0:D].rearrange("p (h e) -> p h e", e=HD),
                                  rden.unsqueeze(2).to_broadcast([T, HEADS, HD]), ALU.mult).then_inc(S("a_cn"), 1)
                dve.wait_ge(S("a_ct"), b + 1)
                dve.tensor_copy(cT.rearrange("p a t -> p (a t)"), psum[:, 0, 0:2 * T]).then_inc(S("a_ctc"), 1)
                dve.wait_ge(S("a_o"), b + 1)
                hb = H[:, bass.ds(b, 1), :].rearrange("p a n -> p (a n)")
                dve.scalar_tensor_tensor(out=hb, in0=psum[0:T, 1, 0:D], scalar=small[0:T, 9, bass.ds(b, 1)], in1=hb,
                                         op0=ALU.mult, op1=ALU.add).then_inc(S("a_start"), 1)
            dve.wait_ge(S("a_start"), B + 1)

            deviation(3)
            link(dve.reciprocal(sm(8), sm(5)))
            link(dve.tensor_tensor(XN, XN, wide(sm(8)), ALU.mult))
            xf = XN.rearrange("p b n -> p (b n)")
            t1, t2 = T1.rearrange("p b n -> p (b n)"), T2.rearrange("p b n -> p (b n)")
            for c in range(4):
                n = W8 // 4
                link(fp4(xf[:, c * n:(c + 1) * n], t1[:, 0:n], t1[:, n:2 * n], t1[:, 2 * n:3 * n], t1[:, 3 * n:4 * n],
                         t2[:, 0:n // FB], t2[:, n // FB:2 * n // FB]))
            dve.sem_inc(S("f_start"), 1)
            per = [0]
            with dve.Fori(0, B) as b:
                start = count[0]

                def link_b(ins):
                    per[0] += 1
                    ins.then_inc(S("vec_b"), 1)
                    dve.wait_ge(S("vec_b"), b * N_LINKS + per[0])

                N_LINKS = 19
                dve.wait_ge(S("f_xt"), b + 1)
                dve.tensor_copy(xbT.rearrange("p a t -> p (a t)"), psum[:, 0, 0:2 * T]).then_inc(S("f_xtc"), 1)
                dve.wait_ge(S("f_e"), b + 1)
                link, outer = link_b, link
                half = lambda v: v.rearrange("p (a n) -> p a n", a=2)
                link_b(dve.tensor_scalar(gate, gate, 1.0, None, ALU.add))
                link_b(dve.reciprocal(gate, gate))
                link_b(dve.tensor_tensor(half(gate), psum[0:T, 1:3, 0:I // 2], half(gate), ALU.mult))
                link_b(dve.tensor_tensor(half(hid), psum[0:T, 3:5, 0:I // 2], half(gate), ALU.mult))
                fp4(hid, qa, qc, qd, qe, bmax[:, 0, :], bmax[:, 1, :]).then_inc(S("f_q"), 1)
                assert per[0] == N_LINKS, per[0]
                dve.wait_ge(S("f_o"), b + 1)
                hb = H[:, bass.ds(b, 1), :].rearrange("p a n -> p (a n)")
                dve.tensor_tensor(hb, psum[0:T, 6, 0:D], hb, ALU.add).then_inc(S("f_start"), 1)

    return nc


def kernel(x, cls_tok, L0_tok_W, L0_attn_in_proj_w, L0_attn_in_proj_b, L0_attn_out_w, L0_attn_out_b,
           L0_ffn_w_gate, L0_ffn_w_up, L0_ffn_w_down):
    import numpy as np
    import concourse.bacc as bacc
    from concourse.bass_utils import run_bass_kernel_spmd as run

    s = 16
    x = np.asarray(x)
    xT = x.reshape(B, 8, s, 8, s, 3).transpose(2, 4, 5, 0, 1, 3).reshape(F, B * NP_TOK)
    p = np.arange(P)
    kind0 = (p[:, None] < KG) & (p[:, None] % KG == np.arange(KG)[None])
    kinds = (p[:, None] >= KG) & (p[:, None] % KG == np.arange(KG)[None])
    masks = np.stack([kind0, kinds], 1).astype(np.float32)
    place = np.concatenate([np.arange(1, T), [0]])
    earlier = np.broadcast_to((place[None, :] < place[:, None]), (B, T, T)).astype(np.float32)
    head = (p[:, None] // HD == np.arange(8)[None]).astype(np.float32)
    arrays = {
        "xT": xT, "cls_tok": cls_tok, "w_tok": L0_tok_W, "in_wT": np.asarray(L0_attn_in_proj_w).T,
        "in_b": L0_attn_in_proj_b, "in_bT": np.asarray(L0_attn_in_proj_b).reshape(6, P).T, "out_wT": np.asarray(L0_attn_out_w).T, "out_b": L0_attn_out_b,
        "w_gate": L0_ffn_w_gate, "w_up": L0_ffn_w_up, "w_down": L0_ffn_w_down,
        "feature_masks": masks, "earlier": earlier, "head_mask": head, "identity": np.eye(P, dtype=np.float32),
    }
    arrays = {n + "_in": np.ascontiguousarray(a) for n, a in arrays.items()}
    nc = bacc.Bacc("TRN2", target_bir_lowering=False, num_devices=1)
    args = [nc.dram_tensor(n, a.shape, mybir.dt.from_np(a.dtype), kind="ExternalInput").ap() for n, a in arrays.items()]
    o = nc.dram_tensor("out_0", (B, T, D), F32, kind="ExternalOutput").ap()
    build_vit(nc, *args, o)
    return run(nc, [arrays], core_ids=[0]).results[0]["out_0"]
```

```python
from contextlib import ExitStack

import concourse.bass as bass
from concourse import mybir

ALU = mybir.AluOpType
ACT = mybir.ActivationFunctionType
F32 = mybir.dt.float32
F32R = mybir.dt.float32r
U32 = mybir.dt.uint32
X = mybir.AxisListType.X

P = 128
B = 32
D = 256
T = 65
NP_TOK = T - 1
F = 768
TILES = B * NP_TOK // P
KG = 32
KIND = P // KG
BLOCKS = (512, 256)
UNROLL = 4
QUADS = 4
QW = TILES // QUADS * D
QT = TILES // QUADS
HEADS = 16
HD = D // HEADS
TOPK = 20
I = 704
IC = [(c, min(P, I - c)) for c in range(0, I, P)]
FB = 16
GRID_STEPS = [(0.25, 0.5), (0.75, 0.5), (1.25, 0.5), (1.75, 0.5), (2.5, 1.0), (3.5, 1.0), (5.0, 2.0)]
HI = 0xFFFFF000
EPS = 1e-5


def build_vit(nc, xT, cls_tok, w_tok, in_wT, in_b, in_bT, out_wT, out_b, w_gate, w_up, w_down,
              feature_masks, earlier, head_mask, identity, out):
    with ExitStack() as ctx:
        def sb(name, shape, dt=F32):
            return ctx.enter_context(nc.sbuf_tensor(name, shape, dt))

        def sem(name):
            return ctx.enter_context(nc.semaphore(name))

        W8 = B * D
        work = sb("work", [P, 4 * W8])
        psum = ctx.enter_context(nc.psum_tensor("psum", [P, 8, 512], F32))
        ident = sb("ident", [P, P])
        weights = sb("weights", [P, 3 * 2 * D + 2 * D + 4 * I + len(IC) * D])

        def quads(at):
            return work[:, at:at + QUADS * QW].rearrange("p (q n) -> p q n", q=QUADS)
        total, back, middle, _, acc, first = (quads(n * QUADS * QW) for n in range(6))
        restore = sb("restore", [P, QUADS, QW], F32R)
        ident_r = sb("ident_r", [P, P], F32R)
        raw = work[:, 24576:24576 + B * NP_TOK]
        upper = work[:, 26624:26624 + B * NP_TOK]
        tok_split = sb("tok_split", [P, B * NP_TOK], F32R)
        NG = F // KG
        wsplit = weights[:, 0:NG * D].rearrange("p (g n) -> p g n", g=NG)
        wraw = work[:, 0:NG * D].rearrange("p (g n) -> p g n", g=NG)
        wup = work[:, W8:W8 + NG * D].rearrange("p (g n) -> p g n", g=NG)
        wrow = sb("wrow", [P, UNROLL, 2 * D], F32R)
        masks = sb("masks", [P, 2, KG])

        def rows(k):
            return work[0:T, k * W8:(k + 1) * W8].rearrange("p (b n) -> p b n", b=B)
        H, XN, T1, T2 = rows(0), rows(1), rows(2), rows(3)

        small = sb("small", [P, 18, B])
        sm = lambda k: small[0:T, k, :]
        lanes = sb("lanes", [P, B * 16])
        wq = weights[:, 0:1536].rearrange("p (a n) -> p a n", a=2)
        wo = weights[:, 1536:2048].rearrange("p (a n) -> p a n", a=2)
        wgu = weights[:, 2048:2048 + 4 * I].rearrange("p (w a n) -> p w a n", w=2, a=2)
        wd = weights[:, 2048 + 4 * I:].rearrange("p (c n) -> p c n", c=len(IC))
        in_bias = sb("in_bias", [P, 6])
        row_bias = sb("row_bias", [1, 2, D])
        ones = sb("ones", [P, T])
        hmask = sb("hmask", [P, 8])

        sems = {}
        def S(name):
            if name not in sems:
                sems[name] = sem(name)
            return sems[name]

        GROUPS = [n // KG for n in BLOCKS]
        PER_GROUP = KG // UNROLL
        NSTEP = UNROLL * QUADS
        LAG = 3
        BANKS = QT * D // 512

        def steps(eng, group, slot):
            turn = lambda c: group * PER_GROUP + c
            for s in range(NSTEP):
                slot(turn(0), s, True, lambda n: s >= n)
            with eng.Fori(1, PER_GROUP) as c:
                for s in range(NSTEP):
                    slot(turn(c), s, True, lambda n: True)
            for s in range(LAG):
                slot(turn(PER_GROUP), s, False, lambda n: s < n)

        at = [3 * W8]
        def scratch(parts, *shape):
            n = 1
            for x in shape:
                n *= x
            v = work[0:parts, at[0]:at[0] + n]
            at[0] += n
            if len(shape) == 2:
                v = v.rearrange("p (a b) -> p a b", a=shape[0])
            if len(shape) == 3:
                v = v.rearrange("p (a b c) -> p a b c", a=shape[0], b=shape[1])
            return v
        xb = scratch(T, D)
        xbT = scratch(P, 2, T)
        qT = scratch(P, 2, T)
        kT = scratch(P, 2, T)
        kM = scratch(P, 2, 8, T)
        vS = scratch(T, D)
        sc = scratch(T, HEADS, T)
        pT = scratch(T, HEADS, T)
        cn = scratch(T, D)
        cT = scratch(P, 2, T)
        mx = scratch(T, HEADS)
        den = scratch(T, HEADS)
        rden = scratch(T, HEADS)
        assert at[0] <= 4 * W8
        at[0] = 3 * W8 + D + 2 * T
        gate = scratch(T, I)
        hid = scratch(T, I)
        qa, qc, qd, qe = (scratch(T, I) for _ in range(4))
        hT = scratch(P, len(IC), T)
        bmax = scratch(T, 2, I // FB)
        assert at[0] <= 4 * W8
        at[0] = 2 * W8
        wld, wa, wc, wdd, we = (scratch(P, 1536) for _ in range(5))
        wmax = scratch(P, 2, 96)
        at[0] = 2 * W8
        earl, gt, eq = (scratch(B, T, T) for _ in range(3))
        tokE = sb("tokE", [B, 3, T])

        block = ctx.enter_context(nc.Block())

        @block.sync
        def _(sp):
            for j in range(KIND):
                sp.dma_start(wraw[KG * j:KG * (j + 1), :, :],
                             w_tok.rearrange("(g k) n -> k g n", k=KG)).then_inc(S("w_dma"), 16)
            sp.dma_start(masks[:, :, :], feature_masks).then_inc(S("const_dma"), 16)
            sp.dma_start(ident[:, :], identity).then_inc(S("const_dma"), 16)
            sp.dma_start(hmask[:, :], head_mask).then_inc(S("const_dma"), 16)
            sp.dma_start(in_bias[:, :], in_bT).then_inc(S("const_dma"), 16)
            sp.dma_start(row_bias[:, 0, :], in_b[2 * D:3 * D].rearrange("(a n) -> a n", a=1)).then_inc(S("const_dma"), 16)
            sp.dma_start(row_bias[:, 1, :], out_b.rearrange("(a n) -> a n", a=1)).then_inc(S("const_dma"), 16)
            g0 = 0
            for n in GROUPS:
                with sp.Fori(0, n) as g:
                    sp.wait_ge(S("raw_free"), g + (g0 + 1))
                    for j in range(KIND):
                        sp.dma_start(raw[KG * j:KG * (j + 1), :],
                                     xT[bass.ds((g + g0) * KG, KG), :]).then_inc(S("raw_dma"), 16)
                g0 += n
            sp.wait_ge(S("tokens_done"), 1)
            t = acc.rearrange("p q (t n) -> p (q t) n", n=D)
            for half in range(2):
                sp.dma_start(H[0:NP_TOK, half:B:2, :],
                             t[NP_TOK * half:NP_TOK * (half + 1), :, :]).then_inc(S("h_dma"), 16)
            sp.dma_start(H[NP_TOK:T, :, :], cls_tok[0].unsqueeze(1).to_broadcast([1, B, D])).then_inc(S("h_dma"), 16)
            sp.dma_start(wq[:, :, :], in_wT.rearrange("(a p) n -> p a n", p=P)).then_inc(S("h_dma"), 16)
            sp.dma_start(wo[:, :, :], out_wT.rearrange("(a p) n -> p a n", p=P)).then_inc(S("h_dma"), 16)
            for w, src in enumerate((w_gate, w_up, w_down)):
                sp.wait_ge(S("wld_free"), w + 1)
                if w < 2:
                    d3 = wld.rearrange("p (c n) -> p c n", c=len(IC))
                    sp.dma_start(d3[:, 0:5, :], src[0:5 * P, :].rearrange("(c p) n -> p c n", p=P)).then_inc(S("wld_dma"), 16)
                    sp.dma_start(d3[0:I - 5 * P, 5, :], src[5 * P:I, :]).then_inc(S("wld_dma"), 16)
                else:
                    sp.dma_start(wld[:, 0:2 * I].rearrange("p (a n) -> p a n", a=2),
                                 src.rearrange("(a p) n -> p a n", p=P)).then_inc(S("wld_dma"), 32)
            sp.wait_ge(S("lanes_free"), 1)
            sp.dma_start(earl[:, :, :], earlier).then_inc(S("earl_dma"), 16)
            sp.wait_ge(S("f_start"), B + 1)
            o = out.rearrange("b t n -> t b n")
            sp.dma_start(o[0:1, :, :], H[NP_TOK:T, :, :]).then_inc(S("out_dma"), 16)
            sp.dma_start(o[1:T, :, :], H[0:NP_TOK, :, :]).then_inc(S("out_dma"), 16)
            sp.wait_ge(S("out_dma"), 32)

        def attention_act(act):
            with act.Fori(0, B) as b:
                act.wait_ge(S("a_start"), b + 1)
                act.activation(xb, XN[:, bass.ds(b, 1), :].rearrange("p a n -> p (a n)"), ACT.Copy).then_inc(S("a_x"), 1)
                act.wait_ge(S("a_qkv"), b + 1)
                for o in range(2):
                    act.activation(qT[:, o, :], psum[:, 1, o * T:(o + 1) * T], ACT.Identity, bias=in_bias[:, o:o + 1])
                    act.activation(kT[:, o, :], psum[:, 1, (2 + o) * T:(3 + o) * T], ACT.Identity,
                                   bias=in_bias[:, 2 + o:3 + o])
                act.activation(vS, psum[0:T, 2, 0:D], ACT.Copy).then_inc(S("a_kv"), 1)
                act.wait_ge(S("a_sub"), b + 1)
                act.activation(sc, sc, ACT.Exp, scale=float(HD) ** -0.5).then_inc(S("a_exp"), 1)
                act.wait_ge(S("a_pt"), b + 1)
                act.activation(pT.rearrange("p (g h) t -> p g (h t)", g=4), psum[0:T, 3:7, 0:4 * T],
                               ACT.Copy).then_inc(S("a_ptc"), 1)

        def ffn_act(act):
            with act.Fori(0, B) as b:
                act.wait_ge(S("f_start"), b + 1)
                act.activation(xb, XN[:, bass.ds(b, 1), :].rearrange("p a n -> p (a n)"), ACT.Copy).then_inc(S("f_x"), 1)
                act.wait_ge(S("f_gu"), b + 1)
                act.activation(gate.rearrange("p (a n) -> p a n", a=2), psum[0:T, 1:3, 0:I // 2],
                               ACT.Exp, scale=-1.0).then_inc(S("f_e"), 1)
                act.wait_ge(S("f_ht"), b + 1)
                act.activation(hT[:, 0:5, :], psum[:, 5, 0:5 * T].rearrange("p (c t) -> p c t", c=5), ACT.Copy)
                act.activation(hT[0:I - 5 * P, 5, :], psum[0:I - 5 * P, 5, 5 * T:6 * T], ACT.Copy).then_inc(S("f_htc"), 1)

        @block.scalar
        def _(act):
            g0 = 0
            act.wait_ge(S("w_split"), 4)
            act.wait_ge(S("const_dma"), 96)
            for n in GROUPS:
                with act.Fori(0, n) as g:
                    act.wait_ge(S("split_hi"), g + (g0 + 1))
                    act.activation(tok_split[0:2 * KG, :], upper[0:2 * KG, :], ACT.Copy).then_inc(S("split_act"), 1)
                    with act.Fori(0, PER_GROUP) as c:
                        for u in range(UNROLL):
                            act.wait_ge(S("rest_ready"), (((g + g0) * PER_GROUP + c) * UNROLL + (u + 1)) * QUADS)
                            for part in range(2):
                                ins = act.activation(wrow[:, u, part * D:(part + 1) * D],
                                                     wsplit[:, bass.ds(g + g0, 1), :].rearrange("p a n -> p (a n)"),
                                                     ACT.Copy, scale=masks[:, part, bass.ds(c * UNROLL + u, 1)])
                            ins.then_inc(S("row_ready"), 1)
                g0 += n
            for k in range(3):
                act.wait_ge(S("sqrt_in"), k + 1)
                act.activation(sm(1), sm(0), ACT.Sqrt).then_inc(S("sqrt_out"), 1)
                if k == 1:
                    attention_act(act)
            ffn_act(act)

        @block.gpsimd
        def _(pool):
            def slot(turn, s, new, back_n):
                if not new:
                    return
                i, q = turn * NSTEP + s, s % QUADS
                if s % 2 == 0:
                    pool.wait_ge(S("back_ready"), i + 1)
                    pool.tensor_tensor(middle[:, q, :], total[:, q, :], back[:, q, :], ALU.add).then_inc(S("middle_pool"), 1)
                    pool.wait_ge(S("middle_pool"), turn * (NSTEP // 2) + (s // 2 + 1))
                else:
                    pool.wait_ge(S("middle_dve"), turn * (NSTEP // 2) + (s // 2 + 1))
                pool.tensor_tensor(restore[:, q, :], acc[:, q, :], middle[:, q, :], ALU.subtract).then_inc(S("restore_ready"), 1)
            g0 = 0
            for n in GROUPS:
                with pool.Fori(0, n) as g:
                    steps(pool, g + g0, slot)
                g0 += n

        @block.tensor
        def _(pe):
            pe.wait_ge(S("ident_ready"), 1)

            def bank(s, n):
                return psum[:, (s % QUADS) * BANKS + n, :]

            def products(s, part):
                for t in range(QT):
                    q = s % QUADS
                    last = pe.matmul(bank(s, t // 2)[:, (t % 2) * D:(t % 2 + 1) * D],
                                     tok_split[:, (q * QT + t) * P:(q * QT + t + 1) * P],
                                     wrow[:, s // QUADS % UNROLL, part * D:(part + 1) * D],
                                     start=(part == 0 and t % 2 == 0), stop=False, skip_group_check=True)
                return last

            def slot(turn, s, new, back_n):
                i = turn * NSTEP + s
                if new:
                    if s % QUADS == 0:
                        pe.wait_ge(S("row_ready"), turn * UNROLL + (s // QUADS + 1))
                    pe.wait_ge(S("acc_ready"), i + (1 + 4 * blk))
                    products(s, 0).then_inc(S("products"), 1)
                if back_n(3):
                    pe.wait_ge(S("restore_ready"), i - (3 - 1))
                    for n in range(BANKS):
                        last = pe.matmul(bank(s - 3, n), ident_r[:, :], restore[:, (s - 3) % QUADS, n * 512:(n + 1) * 512],
                                         start=False, stop=True, skip_group_check=True)
                    last.then_inc(S("rest_ready"), 1)
                if back_n(1):
                    pe.wait_ge(S("back_ready"), i)
                    for n in range(BANKS):
                        pe.matmul(bank(s - 1, n), ident[:, :], back[:, (s - 1) % QUADS, n * 512:(n + 1) * 512],
                                  start=False, stop=False, skip_group_check=True)
                    products(s - 1, 1)

            g0 = 0
            for blk, n in enumerate(GROUPS):
                with pe.Fori(0, n) as g:
                    pe.wait_ge(S("split_act"), g + (g0 + 1))
                    pe.wait_ge(S("split_dve"), g + (g0 + 1))
                    steps(pe, g + g0, slot)
                g0 += n
            for w in range(3):
                pe.wait_ge(S("w_quant"), w + 1)
                if w < 2:
                    v = wld.rearrange("p (c n) -> p c n", c=len(IC))
                    for a in range(2):
                        for c, (_, m) in enumerate(IC):
                            last = pe.transpose(psum[:, a * 2 + c // 4, (c % 4) * P:(c % 4) * P + m],
                                                v[0:m, c, a * P:(a + 1) * P], ident[0:m, 0:m])
                else:
                    v = wld[:, 0:2 * I].rearrange("p (a n) -> p a n", a=2)
                    for c, (o, m) in enumerate(IC):
                        for a in range(2):
                            last = pe.transpose(psum[0:m, c // 2, (c % 2) * D + a * P:(c % 2) * D + (a + 1) * P],
                                                v[:, a, o:o + m], ident[:, :])
                last.then_inc(S("w_turned"), 1)
            pe.wait_ge(S("energy"), 1)
            pe.transpose(psum[0:B, 0, 0:T], sm(4), ident[0:T, 0:T]).then_inc(S("energy_t"), 1)
            pe.wait_ge(S("picked"), 1)
            pe.transpose(psum[0:T, 1, 0:B], tokE[:, 2, :], ident[0:B, 0:B]).then_inc(S("picked_t"), 1)
            for r in range(2):
                pe.wait_ge(S("banks_read"), r + 1)
                for n in range(8):
                    last = pe.matmul(psum[0:T, n, :], ones[0:T, :],
                                     XN.rearrange("p b n -> p (b n)")[:, (8 * r + n) * 512:(8 * r + n + 1) * 512],
                                     start=True, stop=True)
                last.then_inc(S("mean_sum"), 1)
            with pe.Fori(0, B) as b:
                pe.wait_ge(S("a_x"), b + 1)
                for a in range(2):
                    last = pe.transpose(psum[:, 0, a * T:(a + 1) * T], xb[:, a * P:(a + 1) * P], ident[0:T, 0:T])
                last.then_inc(S("a_xt"), 1)
                pe.wait_ge(S("a_xtc"), b + 1)
                for o in range(4):
                    for a in range(2):
                        pe.matmul(psum[:, 1, o * T:(o + 1) * T], wq[:, a, o * P:(o + 1) * P], xbT[:, a, :],
                                  start=(a == 0), stop=(a == 1))
                for a in range(2):
                    pe.matmul(psum[0:T, 2, 0:D], xbT[:, a, :], wq[:, a, 2 * D:3 * D], start=(a == 0), stop=False)
                pe.matmul(psum[0:T, 2, 0:D], ones[0:1, :], row_bias[:, 0, :], start=False, stop=True).then_inc(S("a_qkv"), 1)
                pe.wait_ge(S("a_km"), b + 1)
                for g in range(4):
                    last = pe.matmul(psum[0:T, 3 + g, 0:4 * T], qT[:, g // 2, :],
                                     kM[:, g // 2, (g % 2) * 4:(g % 2) * 4 + 4, :].rearrange("p h t -> p (h t)"),
                                     start=True, stop=True)
                last.then_inc(S("a_sc"), 1)
                pe.wait_ge(S("a_exp"), b + 1)
                for h in range(HEADS):
                    last = pe.transpose(psum[0:T, 3 + h // 4, (h % 4) * T:(h % 4 + 1) * T], sc[:, h, :], ident[0:T, 0:T])
                last.then_inc(S("a_pt"), 1)
                pe.wait_ge(S("a_ptc"), b + 1)
                for h in range(HEADS):
                    last = pe.matmul(psum[0:T, 7, h * HD:(h + 1) * HD], pT[:, h, :], vS[:, h * HD:(h + 1) * HD],
                                     start=True, stop=True)
                last.then_inc(S("a_pv"), 1)
                pe.wait_ge(S("a_cn"), b + 1)
                for a in range(2):
                    last = pe.transpose(psum[:, 0, a * T:(a + 1) * T], cn[:, a * P:(a + 1) * P], ident[0:T, 0:T])
                last.then_inc(S("a_ct"), 1)
                pe.wait_ge(S("a_ctc"), b + 1)
                for a in range(2):
                    pe.matmul(psum[0:T, 1, 0:D], cT[:, a, :], wo[:, a, :], start=(a == 0), stop=False)
                pe.matmul(psum[0:T, 1, 0:D], ones[0:1, :], row_bias[:, 1, :], start=False, stop=True).then_inc(S("a_o"), 1)
            with pe.Fori(0, B) as b:
                pe.wait_ge(S("f_x"), b + 1)
                for a in range(2):
                    last = pe.transpose(psum[:, 0, a * T:(a + 1) * T], xb[:, a * P:(a + 1) * P], ident[0:T, 0:T])
                last.then_inc(S("f_xt"), 1)
                pe.wait_ge(S("f_xtc"), b + 1)
                for w in range(2):
                    for n in range(2):
                        for a in range(2):
                            last = pe.matmul(psum[0:T, 1 + 2 * w + n, 0:I // 2], xbT[:, a, :],
                                             wgu[:, w, a, n * (I // 2):(n + 1) * (I // 2)], start=(a == 0), stop=(a == 1))
                last.then_inc(S("f_gu"), 1)
                pe.wait_ge(S("f_q"), b + 1)
                for c, (o, m) in enumerate(IC):
                    last = pe.transpose(psum[0:m, 5, c * T:(c + 1) * T], hid[:, o:o + m], ident[0:T, 0:T])
                last.then_inc(S("f_ht"), 1)
                pe.wait_ge(S("f_htc"), b + 1)
                for c, (_, m) in enumerate(IC):
                    last = pe.matmul(psum[0:T, 6, 0:D], hT[0:m, c, :], wd[0:m, c, :], start=(c == 0), stop=(c == len(IC) - 1))
                last.then_inc(S("f_o"), 1)

        @block.vector
        def _(dve):
            count = [0]

            def link(ins):
                count[0] += 1
                ins.then_inc(S("vec"), 1)
                dve.wait_ge(S("vec"), count[0])

            dve.sem_inc(S("raw_free"), 1)
            dve.sem_inc(S("rest_ready"), UNROLL * QUADS)
            dve.wait_ge(S("const_dma"), 96)
            dve.tensor_copy(ident_r[:, :], ident[:, :]).then_inc(S("ident_ready"), 1)
            dve.wait_ge(S("w_dma"), 64)
            link(dve.tensor_scalar(wup.bitcast(U32), wraw.bitcast(U32), HI, None, ALU.bitwise_and))
            for j in range(KIND):
                r = slice(KG * j, KG * (j + 1))
                if j % 2 == 0:
                    dve.tensor_copy(wsplit[r], wup[r]).then_inc(S("w_split"), 1)
                else:
                    dve.tensor_tensor(wsplit[r], wraw[r], wup[r], ALU.subtract).then_inc(S("w_split"), 1)
            dve.wait_ge(S("w_split"), 4)

            def rest(s):
                b = s % QUADS * BANKS
                return psum[:, b:b + BANKS, :]

            def banks(v, s):
                return v[:, s % QUADS, :].rearrange("p (k n) -> p k n", n=512)

            def slot(turn, s, new, back_n):
                i = turn * NSTEP + s
                q = s % QUADS
                if new:
                    dve.wait_ge(S("products"), i + 1)
                    dve.wait_ge(S("acc_ready"), i + (1 + 4 * blk))
                    dve.tensor_tensor(banks(total, s), rest(s), banks(acc, s), ALU.add).then_inc(S("total_ready"), 1)
                if back_n(3):
                    dve.wait_ge(S("rest_ready"), i + (UNROLL * QUADS + 1 - 3))
                    dve.tensor_tensor(banks(acc, s - 3), rest(s - 3), banks(total, s - 3),
                                      ALU.add).then_inc(S("acc_ready"), 1)
                if back_n(1) and s % 2 == 0:
                    dve.wait_ge(S("back_ready"), i)
                    dve.tensor_tensor(middle[:, (s - 1) % QUADS, :], total[:, (s - 1) % QUADS, :],
                                      back[:, (s - 1) % QUADS, :], ALU.add).then_inc(S("middle_dve"), 1)
                if new:
                    dve.wait_ge(S("total_ready"), i + 1)
                    dve.tensor_tensor(back[:, q, :], acc[:, q, :], total[:, q, :], ALU.subtract).then_inc(S("back_ready"), 1)

            g0 = 0
            for blk, n in enumerate(GROUPS):
                dve.memset(acc, 0.0).then_inc(S("acc_ready"), 4)
                with dve.Fori(0, n) as g:
                    dve.wait_ge(S("raw_dma"), (g + (g0 + 1)) * 64)
                    dve.tensor_scalar(upper.bitcast(U32), raw.bitcast(U32), HI, None, ALU.bitwise_and).then_inc(S("split_hi"), 1)
                    dve.wait_ge(S("split_hi"), g + (g0 + 1))
                    dve.tensor_tensor(tok_split[2 * KG:P, :], raw[2 * KG:P, :], upper[2 * KG:P, :],
                                      ALU.subtract).then_inc(S("split_dve"), 1)
                    dve.wait_ge(S("split_dve"), g + (g0 + 1))
                    dve.sem_inc(S("raw_free"), 1)
                    steps(dve, g + g0, slot)
                g0 += n
                done = g0 * PER_GROUP * NSTEP + 4 * (blk + 1)
                dve.wait_ge(S("acc_ready"), done)
                if blk == 0:
                    link(dve.tensor_copy(first, acc))
                else:
                    dve.tensor_tensor(acc, first, acc, ALU.add).then_inc(S("tokens_done"), 1)

            def fp4(x, a, c, d, e, top, scale):
                n = x.free_size() // FB
                blocks = lambda v: v.rearrange("p (b s) -> p b s", s=FB)
                wide = lambda v: v.unsqueeze(2).to_broadcast([v.shape[0], n, FB])
                link(dve.tensor_reduce(top, blocks(x), X, ALU.max, apply_absolute_value=True))
                link(dve.tensor_scalar(top, top, 1.0 / 6.0, 1e-12, ALU.mult, ALU.max))
                link(dve.reciprocal(scale, top))
                link(dve.tensor_scalar(a.bitcast(U32), x.bitcast(U32), 0x7FFFFFFF, None, ALU.bitwise_and))
                link(dve.tensor_tensor(blocks(a), blocks(a), wide(scale), ALU.mult))
                link(dve.tensor_scalar(c, a, GRID_STEPS[0][0], None, ALU.is_gt))
                for mid, _ in GRID_STEPS[1:4]:
                    link(dve.scalar_tensor_tensor(out=c, in0=a, scalar=mid, in1=c, op0=ALU.is_gt, op1=ALU.add))
                link(dve.tensor_scalar(d, a, GRID_STEPS[4][0], None, ALU.is_gt))
                link(dve.scalar_tensor_tensor(out=d, in0=a, scalar=GRID_STEPS[5][0], in1=d, op0=ALU.is_gt, op1=ALU.add))
                link(dve.tensor_scalar(e, a, GRID_STEPS[6][0], 2.0, ALU.is_gt, ALU.mult))
                link(dve.tensor_tensor(d, d, e, ALU.add))
                link(dve.scalar_tensor_tensor(out=c, in0=c, scalar=0.5, in1=d, op0=ALU.mult, op1=ALU.add))
                link(dve.tensor_tensor(blocks(c), blocks(c), wide(top), ALU.mult))
                return dve.scalar_tensor_tensor(out=x.bitcast(U32), in0=x.bitcast(U32), scalar=0x80000000,
                                                in1=c.bitcast(U32), op0=ALU.bitwise_and, op1=ALU.bitwise_or)

            dve.wait_ge(S("tokens_done"), 1)
            dve.wait_ge(S("h_dma"), 80)
            dve.memset(ones[:, :], 1.0)
            link(dve.memset(wld, 0.0))
            dve.sem_inc(S("wld_free"), 1)
            for w in range(3):
                dve.wait_ge(S("wld_dma"), 32 * (w + 1))
                n = 6 * D if w < 2 else 2 * I
                fp4(wld[:, 0:n], wa[:, 0:n], wc[:, 0:n], wdd[:, 0:n], we[:, 0:n],
                    wmax[:, 0, 0:n // FB], wmax[:, 1, 0:n // FB]).then_inc(S("w_quant"), 1)
                dve.wait_ge(S("w_turned"), w + 1)
                if w < 2:
                    for a in range(2):
                        dve.tensor_copy(wgu[:, w, a, 0:512], psum[:, a * 2, :])
                        last = dve.tensor_copy(wgu[:, w, a, 512:I], psum[:, a * 2 + 1, 0:I - 512])
                else:
                    for c, (_, m) in enumerate(IC):
                        last = dve.tensor_copy(wd[0:m, c, :], psum[0:m, c // 2, (c % 2) * D:(c % 2 + 1) * D])
                link(last)
                dve.sem_inc(S("wld_free"), 1)

            def wide(v, n=D):
                return v.unsqueeze(2).to_broadcast([T, v.shape[1], n])

            def root(k, n):
                y, yh, yl, r, t = sm(1), sm(13), sm(14), sm(15), sm(16)
                dve.sem_inc(S("sqrt_in"), 1)
                dve.wait_ge(S("sqrt_out"), n)
                link(dve.tensor_scalar(yh.bitcast(U32), y.bitcast(U32), HI, None, ALU.bitwise_and))
                link(dve.tensor_tensor(yl, y, yh, ALU.subtract))
                link(dve.tensor_tensor(t, yh, yh, ALU.mult))
                link(dve.tensor_tensor(r, sm(0), t, ALU.subtract))
                link(dve.scalar_tensor_tensor(out=t, in0=yh, scalar=2.0, in1=yl, op0=ALU.mult, op1=ALU.mult))
                link(dve.tensor_tensor(r, r, t, ALU.subtract))
                link(dve.tensor_tensor(t, yl, yl, ALU.mult))
                link(dve.tensor_tensor(r, r, t, ALU.subtract))
                link(dve.tensor_scalar(t, y, 2.0, 1e-30, ALU.mult, ALU.max))
                link(dve.reciprocal(t, t))
                link(dve.tensor_tensor(r, r, t, ALU.mult))
                link(dve.tensor_tensor(sm(k), y, r, ALU.add))

            def mean_lanes(src, k):
                ln = lanes[0:T, :].rearrange("p (b l) -> p b l", l=16)
                link(dve.tensor_reduce(ln, src.rearrange("p b (i l) -> p b l i", l=16), X, ALU.add))
                link(dve.tensor_tensor(ln[:, :, 0:4], ln[:, :, 0:4], ln[:, :, 4:8], ALU.add))
                link(dve.tensor_tensor(ln[:, :, 8:12], ln[:, :, 8:12], ln[:, :, 12:16], ALU.add))
                link(dve.tensor_tensor(ln[:, :, 0:4], ln[:, :, 0:4], ln[:, :, 8:12], ALU.add))
                link(dve.tensor_tensor(ln[:, :, 0:4:2], ln[:, :, 0:4:2], ln[:, :, 1:4:2], ALU.add))
                link(dve.tensor_tensor(ln[:, :, 0:1], ln[:, :, 0:1], ln[:, :, 2:3], ALU.add))
                link(dve.tensor_scalar(sm(k), ln[:, :, 0], 1.0 / D, None, ALU.mult))

            def squares(src, k):
                link(dve.tensor_tensor(T1, src, src, ALU.mult))
                w8 = lanes[0:T, 0:8 * B].rearrange("p (b w) -> p b w", w=8)
                link(dve.tensor_reduce(w8, T1.rearrange("p b (w s) -> p b w s", s=32), X, ALU.add))
                link(dve.tensor_reduce(sm(k), w8, X, ALU.add))

            def deviation(n):
                mean_lanes(H, 2)
                link(dve.tensor_tensor(XN, H, wide(sm(2)), ALU.subtract))
                squares(XN, 3)
                link(dve.tensor_scalar(sm(0), sm(3), 1.0 / D, EPS, ALU.mult, ALU.add))
                root(5, n)

            deviation(1)
            sh, sl, rs = sm(6), sm(7), sm(8)
            link(dve.tensor_scalar(sh.bitcast(U32), sm(5).bitcast(U32), HI, None, ALU.bitwise_and))
            link(dve.tensor_tensor(sl, sm(5), sh, ALU.subtract))
            link(dve.reciprocal(rs, sm(5)))
            for c in range(4):
                i = slice(8 * c, 8 * c + 8)
                d = XN[:, i, :]
                q0, qh, ql, pr = T1[:, 0:8, :], T1[:, 8:16, :], T1[:, 16:24, :], T1[:, 24:32, :]
                wsh, wsl, wrs = (wide(v[:, i]) for v in (sh, sl, rs))
                rem = T2[:, 0:8, :]
                link(dve.tensor_tensor(q0, d, wrs, ALU.mult))
                link(dve.tensor_scalar(qh.bitcast(U32), q0.bitcast(U32), HI, None, ALU.bitwise_and))
                link(dve.tensor_tensor(ql, q0, qh, ALU.subtract))
                link(dve.tensor_tensor(pr, qh, wsh, ALU.mult))
                link(dve.tensor_tensor(rem, d, pr, ALU.subtract))
                for qx, sx in ((qh, wsl), (ql, wsh), (ql, wsl)):
                    link(dve.tensor_tensor(pr, qx, sx, ALU.mult))
                    link(dve.tensor_tensor(rem, rem, pr, ALU.subtract))
                link(dve.tensor_tensor(rem, rem, wrs, ALU.mult))
                link(dve.tensor_tensor(d, q0, rem, ALU.add))
            squares(XN, 0)
            root(4, 2)
            dve.sem_inc(S("energy"), 1)
            dve.sem_inc(S("lanes_free"), 1)

            dve.wait_ge(S("energy_t"), 1)
            link(dve.tensor_copy(tokE[:, 0, :], psum[0:B, 0, 0:T]))
            ej = tokE[:, 0, :].unsqueeze(1).to_broadcast([B, T, T])
            ei = tokE[:, 0, :].unsqueeze(2).to_broadcast([B, T, T])
            dve.wait_ge(S("earl_dma"), 16)
            dve.tensor_tensor(gt, ej, ei, ALU.is_gt)
            link(dve.tensor_tensor(eq, ej, ei, ALU.is_equal))
            link(dve.tensor_tensor(eq, eq, earl, ALU.mult))
            link(dve.tensor_tensor(gt, gt, eq, ALU.add))
            link(dve.tensor_reduce(tokE[:, 1, :], gt, X, ALU.add))
            dve.tensor_scalar(tokE[:, 2, :], tokE[:, 1, :], float(TOPK), None, ALU.is_lt).then_inc(S("picked"), 1)
            dve.wait_ge(S("picked_t"), 1)
            link(dve.tensor_copy(sm(9), psum[0:T, 1, 0:B]))
            dve.sem_inc(S("banks_read"), 1)
            link(dve.tensor_scalar(sm(10), sm(9), -1.0 / T, 1.0 / T, ALU.mult, ALU.add))
            for r in range(2):
                dve.wait_ge(S("mean_sum"), r + 1)
                i = slice(16 * r, 16 * r + 16)
                ps = psum[0:T, :, :].rearrange("p k (b n) -> p (k b) n", n=D)
                ins = dve.tensor_tensor(T1[:, i, :], ps, wide(sm(10)[:, i]), ALU.mult)
                link(ins)
                dve.sem_inc(S("banks_read"), 1)
            link(dve.tensor_tensor(H, H, T1, ALU.add))
            dve.sem_inc(S("a_start"), 1)

            with dve.Fori(0, B) as b:
                dve.wait_ge(S("a_xt"), b + 1)
                dve.tensor_copy(xbT.rearrange("p a t -> p (a t)"), psum[:, 0, 0:2 * T]).then_inc(S("a_xtc"), 1)
                dve.wait_ge(S("a_kv"), b + 1)
                for o in range(2):
                    ins = dve.tensor_tensor(kM[:, o, :, :], kT[:, o, :].unsqueeze(1).to_broadcast([P, 8, T]),
                                            hmask[:, :].unsqueeze(2).to_broadcast([P, 8, T]), ALU.mult)
                ins.then_inc(S("a_km"), 1)
                dve.wait_ge(S("a_sc"), b + 1)
                s4 = psum[0:T, 3:7, 0:4 * T].rearrange("p g (h t) -> p g h t", t=T)
                dve.tensor_reduce(mx.rearrange("p (g h) -> p g h", g=4), s4, X, ALU.max).then_inc(S("a_mx"), 1)
                dve.wait_ge(S("a_mx"), b + 1)
                for g in range(4):
                    ins = dve.tensor_tensor(sc[:, 4 * g:4 * g + 4, :], s4[:, g, :, :],
                                            mx[:, 4 * g:4 * g + 4].unsqueeze(2).to_broadcast([T, 4, T]), ALU.subtract)
                ins.then_inc(S("a_sub"), 1)
                dve.wait_ge(S("a_exp"), b + 1)
                dve.tensor_reduce(den, sc, X, ALU.add).then_inc(S("a_den"), 1)
                dve.wait_ge(S("a_den"), b + 1)
                dve.reciprocal(rden, den).then_inc(S("a_rden"), 1)
                dve.wait_ge(S("a_pv"), b + 1)
                dve.wait_ge(S("a_rden"), b + 1)
                dve.tensor_tensor(cn.rearrange("p (h e) -> p h e", e=HD), psum[0:T, 7, 0:D].rearrange("p (h e) -> p h e", e=HD),
                                  rden.unsqueeze(2).to_broadcast([T, HEADS, HD]), ALU.mult).then_inc(S("a_cn"), 1)
                dve.wait_ge(S("a_ct"), b + 1)
                dve.tensor_copy(cT.rearrange("p a t -> p (a t)"), psum[:, 0, 0:2 * T]).then_inc(S("a_ctc"), 1)
                dve.wait_ge(S("a_o"), b + 1)
                hb = H[:, bass.ds(b, 1), :].rearrange("p a n -> p (a n)")
                dve.scalar_tensor_tensor(out=hb, in0=psum[0:T, 1, 0:D], scalar=small[0:T, 9, bass.ds(b, 1)], in1=hb,
                                         op0=ALU.mult, op1=ALU.add).then_inc(S("a_start"), 1)
            dve.wait_ge(S("a_start"), B + 1)

            deviation(3)
            link(dve.reciprocal(sm(8), sm(5)))
            link(dve.tensor_tensor(XN, XN, wide(sm(8)), ALU.mult))
            xf = XN.rearrange("p b n -> p (b n)")
            t1, t2 = T1.rearrange("p b n -> p (b n)"), T2.rearrange("p b n -> p (b n)")
            for c in range(4):
                n = W8 // 4
                link(fp4(xf[:, c * n:(c + 1) * n], t1[:, 0:n], t1[:, n:2 * n], t1[:, 2 * n:3 * n], t1[:, 3 * n:4 * n],
                         t2[:, 0:n // FB], t2[:, n // FB:2 * n // FB]))
            dve.sem_inc(S("f_start"), 1)
            per = [0]
            with dve.Fori(0, B) as b:
                start = count[0]

                def link_b(ins):
                    per[0] += 1
                    ins.then_inc(S("vec_b"), 1)
                    dve.wait_ge(S("vec_b"), b * N_LINKS + per[0])

                N_LINKS = 19
                dve.wait_ge(S("f_xt"), b + 1)
                dve.tensor_copy(xbT.rearrange("p a t -> p (a t)"), psum[:, 0, 0:2 * T]).then_inc(S("f_xtc"), 1)
                dve.wait_ge(S("f_e"), b + 1)
                link, outer = link_b, link
                half = lambda v: v.rearrange("p (a n) -> p a n", a=2)
                link_b(dve.tensor_scalar(gate, gate, 1.0, None, ALU.add))
                link_b(dve.reciprocal(gate, gate))
                link_b(dve.tensor_tensor(half(gate), psum[0:T, 1:3, 0:I // 2], half(gate), ALU.mult))
                link_b(dve.tensor_tensor(half(hid), psum[0:T, 3:5, 0:I // 2], half(gate), ALU.mult))
                fp4(hid, qa, qc, qd, qe, bmax[:, 0, :], bmax[:, 1, :]).then_inc(S("f_q"), 1)
                assert per[0] == N_LINKS, per[0]
                dve.wait_ge(S("f_o"), b + 1)
                hb = H[:, bass.ds(b, 1), :].rearrange("p a n -> p (a n)")
                dve.tensor_tensor(hb, psum[0:T, 6, 0:D], hb, ALU.add).then_inc(S("f_start"), 1)

    return nc


def kernel(x, cls_tok, L0_tok_W, L0_attn_in_proj_w, L0_attn_in_proj_b, L0_attn_out_w, L0_attn_out_b,
           L0_ffn_w_gate, L0_ffn_w_up, L0_ffn_w_down):
    import numpy as np
    import concourse.bacc as bacc
    from concourse.bass_utils import run_bass_kernel_spmd as run

    s = 16
    x = np.asarray(x)
    xT = x.reshape(B, 8, s, 8, s, 3).transpose(2, 4, 5, 0, 1, 3).reshape(F, B * NP_TOK)
    p = np.arange(P)
    kind0 = (p[:, None] < KG) & (p[:, None] % KG == np.arange(KG)[None])
    kinds = (p[:, None] >= KG) & (p[:, None] % KG == np.arange(KG)[None])
    masks = np.stack([kind0, kinds], 1).astype(np.float32)
    place = np.concatenate([np.arange(1, T), [0]])
    earlier = np.broadcast_to((place[None, :] < place[:, None]), (B, T, T)).astype(np.float32)
    head = (p[:, None] // HD == np.arange(8)[None]).astype(np.float32)
    arrays = {
        "xT": xT, "cls_tok": cls_tok, "w_tok": L0_tok_W, "in_wT": np.asarray(L0_attn_in_proj_w).T,
        "in_b": L0_attn_in_proj_b, "in_bT": np.asarray(L0_attn_in_proj_b).reshape(6, P).T, "out_wT": np.asarray(L0_attn_out_w).T, "out_b": L0_attn_out_b,
        "w_gate": L0_ffn_w_gate, "w_up": L0_ffn_w_up, "w_down": L0_ffn_w_down,
        "feature_masks": masks, "earlier": earlier, "head_mask": head, "identity": np.eye(P, dtype=np.float32),
    }
    arrays = {n + "_in": np.ascontiguousarray(a) for n, a in arrays.items()}
    nc = bacc.Bacc("TRN2", target_bir_lowering=False, num_devices=1)
    args = [nc.dram_tensor(n, a.shape, mybir.dt.from_np(a.dtype), kind="ExternalInput").ap() for n, a in arrays.items()]
    o = nc.dram_tensor("out_0", (B, T, D), F32, kind="ExternalOutput").ap()
    build_vit(nc, *args, o)
    return run(nc, [arrays], core_ids=[0]).results[0]["out_0"]
```

```python
from contextlib import ExitStack

import concourse.bass as bass
from concourse import mybir

ALU = mybir.AluOpType
ACT = mybir.ActivationFunctionType
F32 = mybir.dt.float32
F32R = mybir.dt.float32r
U32 = mybir.dt.uint32
X = mybir.AxisListType.X

P = 128
B = 32
D = 256
T = 65
NP_TOK = T - 1
F = 768
TILES = B * NP_TOK // P
KG = 32
KIND = P // KG
BLOCKS = (512, 256)
UNROLL = 4
QUADS = 4
QW = TILES // QUADS * D
QT = TILES // QUADS
HEADS = 16
HD = D // HEADS
TOPK = 20
I = 704
IC = [(c, min(P, I - c)) for c in range(0, I, P)]
FB = 16
MIDS = (0.25, 0.75, 1.25, 1.75, 2.5, 3.5, 5.0)
HI = 0xFFFFF000
EPS = 1e-5


def build_vit(nc, xT, cls_tok, w_tok, in_wT, in_b, in_bT, out_wT, out_b, w_gate, w_up, w_down,
              feature_masks, earlier, head_mask, identity, out):
    with ExitStack() as ctx:
        def sb(name, shape, dt=F32):
            return ctx.enter_context(nc.sbuf_tensor(name, shape, dt))

        def sem(name):
            return ctx.enter_context(nc.semaphore(name))

        W8 = B * D
        NG = F // KG
        QUAD_SET = QUADS * QW
        with ExitStack() as chain_ctx:
            def chain_sb(name, shape, dt=F32):
                return chain_ctx.enter_context(nc.sbuf_tensor(name, shape, dt))
            sums = chain_sb("sums", [P, 3 * QUAD_SET])
            first, acc = (sums[:, n * QUAD_SET:(n + 1) * QUAD_SET].rearrange("p (q n) -> p q n", q=QUADS) for n in (1, 2))
            wraw, wup = (sums[:, n * NG * D:(n + 1) * NG * D].rearrange("p (g n) -> p g n", g=NG) for n in range(2))
            acc_high, acc_low, total_high = (
                chain_sb(name, [P, QUADS, QW], F32R) for name in ("acc_high", "acc_low", "total_high"))
            raw, halves = (chain_sb(name, [P, B * NP_TOK])[:, :] for name in ("raw", "halves"))
        work = sb("work", [P, 4 * W8])
        psum = ctx.enter_context(nc.psum_tensor("psum", [P, 8, 512], F32))
        ident = sb("ident", [P, P])
        weights = sb("weights", [P, 3 * 2 * D + 2 * D + 4 * I + len(IC) * D])
        ident_r = sb("ident_r", [P, P], F32R)
        less_ident = sb("less_ident", [P, P], F32R)
        tok_split = sb("tok_split", [P, B * NP_TOK], F32R)
        wsplit = weights[:, 0:NG * D].rearrange("p (g n) -> p g n", g=NG)
        wrow = sb("wrow", [P, UNROLL, 2 * D], F32R)
        masks = sb("masks", [P, 2, KG])

        def rows(k):
            return work[0:T, k * W8:(k + 1) * W8].rearrange("p (b n) -> p b n", b=B)
        H, XN, T1, T2 = rows(0), rows(1), rows(2), rows(3)

        small = sb("small", [P, 18, B])
        sm = lambda k: small[0:T, k, :]
        lanes = sb("lanes", [P, B * 16])
        wq = weights[:, 0:1536].rearrange("p (a n) -> p a n", a=2)
        wo = weights[:, 1536:2048].rearrange("p (a n) -> p a n", a=2)
        wgu = weights[:, 2048:2048 + 4 * I].rearrange("p (w a n) -> p w a n", w=2, a=2)
        wd = weights[:, 2048 + 4 * I:].rearrange("p (c n) -> p c n", c=len(IC))
        in_bias = sb("in_bias", [P, 6])
        row_bias = sb("row_bias", [1, 2, D])
        ones = sb("ones", [P, T])
        hmask = sb("hmask", [P, 8])

        sems = {}
        def S(name):
            if name not in sems:
                sems[name] = sem(name)
            return sems[name]

        GROUPS = [n // KG for n in BLOCKS]
        PER_GROUP = KG // UNROLL
        NSTEP = UNROLL * QUADS
        LAG = 2
        BANKS = QT * D // 512

        def steps(eng, blk, slot, turn_done=lambda group: None):
            g0, n = sum(GROUPS[:blk]), GROUPS[blk]

            def one(group, ramp, final=False):
                for s in range(NSTEP):
                    slot(group, 0, s, True, lambda n: s >= n or not ramp)
                if not final:
                    turn_done(group)
                with eng.Fori(1, PER_GROUP) as turn:
                    for s in range(NSTEP):
                        slot(group, turn, s, True, lambda n: True)
            final = blk == len(GROUPS) - 1
            one(g0, True)
            with eng.Fori(1, n - final) as g:
                one(g + g0, False)
            if final:
                one(g0 + n - 1, False, True)
            for s in range(LAG):
                slot(g0 + n - 1, PER_GROUP, s, False, lambda n: s < n)

        def opens(turn, s):
            return isinstance(turn, int) and turn == 0 and s < QUADS

        def ffn_turns(eng, front, back):
            front(0, 0)
            with eng.Fori(0, B // 2 - 1) as pairs:
                for p in range(2):
                    front(pairs * 2 + (p + 1), 1 - p)
                    back(pairs * 2 + p, p)
            front(B - 1, 1)
            back(B - 2, 0)
            back(B - 1, 1)

        at = [0]
        def scratch(parts, *shape):
            n = 1
            for x in shape:
                n *= x
            v = work[0:parts, at[0]:at[0] + n]
            at[0] += n
            assert at[0] <= 4 * W8
            if len(shape) == 2:
                v = v.rearrange("p (a b) -> p a b", a=shape[0])
            if len(shape) == 3:
                v = v.rearrange("p (a b c) -> p a b c", a=shape[0], b=shape[1])
            return v

        def pair(parts, *shape):
            return [scratch(parts, *shape) for _ in range(2)]
        at[0] = 2 * W8
        xb, xbT = pair(T, D), pair(P, 2, T)
        after_rows = at[0]
        qT, kT, kM = pair(P, 2, T), pair(P, 2, T), pair(P, 2, 8, T)
        vS, cn, cT = pair(T, D), pair(T, D), pair(P, 2, T)
        sc, pT = pair(T, HEADS, T), pair(T, HEADS, T)
        mx, den, rden = pair(T, HEADS), pair(T, HEADS), pair(T, HEADS)
        at[0] = after_rows
        gate, hid = pair(T, I), pair(T, I)
        qa, qc = pair(T, I), pair(T, I)
        hT, bmax = pair(P, len(IC), T), pair(T, 2, I // FB)
        ffn_out = pair(T, D)
        at[0] = 2 * W8
        wld, wa, wc = (scratch(P, 1536) for _ in range(3))
        wmax = scratch(P, 2, 96)
        at[0] = 2 * W8
        earl, gt, eq = (scratch(B, T, T) for _ in range(3))
        tokE = sb("tokE", [B, 3, T])

        block = ctx.enter_context(nc.Block())

        @block.sync
        def _(sp):
            for j in range(KIND):
                sp.dma_start(wraw[KG * j:KG * (j + 1), :, :],
                             w_tok.rearrange("(g k) n -> k g n", k=KG)).then_inc(S("w_dma"), 16)
            sp.dma_start(masks[:, :, :], feature_masks).then_inc(S("const_dma"), 16)
            sp.dma_start(ident[:, :], identity).then_inc(S("const_dma"), 16)
            sp.dma_start(hmask[:, :], head_mask).then_inc(S("const_dma"), 16)
            sp.dma_start(in_bias[:, :], in_bT).then_inc(S("const_dma"), 16)
            sp.dma_start(row_bias[:, 0, :], in_b[2 * D:3 * D].rearrange("(a n) -> a n", a=1)).then_inc(S("const_dma"), 16)
            sp.dma_start(row_bias[:, 1, :], out_b.rearrange("(a n) -> a n", a=1)).then_inc(S("const_dma"), 16)
            g0 = 0
            for n in GROUPS:
                with sp.Fori(0, n) as g:
                    sp.wait_ge(S("raw_free"), g + (g0 + 1))
                    for j in range(KIND):
                        sp.dma_start(raw[KG * j:KG * (j + 1), :],
                                     xT[bass.ds((g + g0) * KG, KG), :]).then_inc(S("raw_dma"), 16)
                g0 += n
            sp.wait_ge(S("tokens_done"), 1)
            t = acc.rearrange("p q (t n) -> p (q t) n", n=D)
            for half in range(2):
                sp.dma_start(H[0:NP_TOK, half:B:2, :],
                             t[NP_TOK * half:NP_TOK * (half + 1), :, :]).then_inc(S("h_dma"), 16)
            sp.dma_start(H[NP_TOK:T, :, :], cls_tok[0].unsqueeze(1).to_broadcast([1, B, D])).then_inc(S("h_dma"), 16)
            sp.dma_start(wq[:, :, :], in_wT.rearrange("(a p) n -> p a n", p=P)).then_inc(S("h_dma"), 16)
            sp.dma_start(wo[:, :, :], out_wT.rearrange("(a p) n -> p a n", p=P)).then_inc(S("h_dma"), 16)
            for w, src in enumerate((w_gate, w_up, w_down)):
                sp.wait_ge(S("wld_free"), w + 1)
                if w < 2:
                    d3 = wld.rearrange("p (c n) -> p c n", c=len(IC))
                    sp.dma_start(d3[:, 0:5, :], src[0:5 * P, :].rearrange("(c p) n -> p c n", p=P)).then_inc(S("wld_dma"), 16)
                    sp.dma_start(d3[0:I - 5 * P, 5, :], src[5 * P:I, :]).then_inc(S("wld_dma"), 16)
                else:
                    sp.dma_start(wld[:, 0:2 * I].rearrange("p (a n) -> p a n", a=2),
                                 src.rearrange("(a p) n -> p a n", p=P)).then_inc(S("wld_dma"), 32)
            sp.wait_ge(S("lanes_free"), 1)
            sp.dma_start(earl[:, :, :], earlier).then_inc(S("earl_dma"), 16)
            sp.wait_ge(S("f_added"), B)
            o = out.rearrange("b t n -> t b n")
            sp.dma_start(o[0:1, :, :], H[NP_TOK:T, :, :]).then_inc(S("out_dma"), 16)
            sp.dma_start(o[1:T, :, :], H[0:NP_TOK, :, :]).then_inc(S("out_dma"), 16)
            sp.wait_ge(S("out_dma"), 32)

        def attention_act(act):
            with act.Fori(0, B // 2) as pairs:
                for p in range(2):
                    b = pairs * 2 + p
                    act.wait_ge(S(f"a_buffers_free{p}"), pairs + 1)
                    act.activation(xb[p], XN[:, bass.ds(b, 1), :].rearrange("p a n -> p (a n)"),
                                   ACT.Copy).then_inc(S("a_rows"), 1)
                for p in range(2):
                    act.wait_ge(S("a_qkv"), pairs * 2 + (p + 1))
                    for o in range(2):
                        act.activation(qT[p][:, o, :], psum[:, 4 * p, o * T:(o + 1) * T], ACT.Identity,
                                       bias=in_bias[:, o:o + 1])
                        act.activation(kT[p][:, o, :], psum[:, 4 * p, (2 + o) * T:(3 + o) * T], ACT.Identity,
                                       bias=in_bias[:, 2 + o:3 + o])
                    act.activation(vS[p], psum[0:T, 4 * p + 1, 0:D], ACT.Copy).then_inc(S("a_qkv_out"), 1)
                for p in range(2):
                    act.wait_ge(S("a_scores_less_max"), pairs * 2 + (p + 1))
                    act.activation(sc[p], sc[p], ACT.Exp, scale=float(HD) ** -0.5).then_inc(S("a_exp"), 1)
                for p in range(2):
                    act.wait_ge(S("a_exp_turned"), pairs * 2 + (p + 1))
                    act.activation(pT[p].rearrange("p (g h) t -> p g (h t)", g=4), psum[0:T, 4 * p:4 * p + 4, 0:4 * T],
                                   ACT.Copy).then_inc(S("a_exp_turned_out"), 1)

        def ffn_act(act):
            def front(b, p):
                act.activation(xb[p], XN[:, bass.ds(b, 1), :].rearrange("p a n -> p (a n)"), ACT.Copy).then_inc(S("f_rows"), 1)
                act.wait_ge(S("f_rows_turned"), b + 1)
                act.activation(xbT[p].rearrange("p a t -> p (a t)"), psum[:, 4 * p, 0:2 * T], ACT.Copy).then_inc(S("f_rows_turned_out"), 1)
                act.wait_ge(S("f_gate_up"), b + 1)
                act.activation(gate[p].rearrange("p (a n) -> p a n", a=2), psum[0:T, 4 * p + 1:4 * p + 3, 0:I // 2],
                               ACT.Silu).then_inc(S("f_silu"), 1)

            def back(b, p):
                act.wait_ge(S("f_hidden_turned"), b + 1)
                act.activation(hT[p][:, 0:5, :], psum[:, 4 * p + 1, 0:5 * T].rearrange("p (c t) -> p c t", c=5), ACT.Copy)
                act.activation(hT[p][0:I - 5 * P, 5, :], psum[0:I - 5 * P, 4 * p + 1, 5 * T:6 * T],
                               ACT.Copy).then_inc(S("f_hidden_turned_out"), 1)
                act.wait_ge(S("f_down"), b + 1)
                act.activation(ffn_out[p], psum[0:T, 4 * p + 2, 0:D], ACT.Copy).then_inc(S("f_down_out"), 1)

            act.wait_ge(S("ffn_rows"), 1)
            ffn_turns(act, front, back)

        @block.scalar
        def _(act):
            act.wait_ge(S("w_split"), 4)
            act.wait_ge(S("const_dma"), 96)

            def slot(group, turn, s, new, back_n):
                i, q = (group * PER_GROUP + turn) * NSTEP + s, s % QUADS
                if new and q == 0:
                    for part in range(2):
                        ins = act.activation(wrow[:, s // QUADS, part * D:(part + 1) * D],
                                             wsplit[:, bass.ds(group, 1), :].rearrange("p a n -> p (a n)"),
                                             ACT.Copy, scale=masks[:, part, bass.ds(turn * UNROLL + s // QUADS, 1)])
                    ins.then_inc(S("row_ready"), 1)
                if new:
                    act.wait_ge(S("acc_ready"), i + (1 + 4 * blk))
                    if opens(turn, s):
                        act.wait_ge(S("split_dve"), group + 1)
                        part = slice(q * QT * P, (q + 1) * QT * P)
                        act.activation(tok_split[:, part], halves[:, part], ACT.Copy).then_inc(S("quad_split"), 1)
                    act.activation(acc_high[:, q, :], acc[:, q, :], ACT.Copy).then_inc(S("acc_high_ready"), 1)

            for blk in range(len(GROUPS)):
                steps(act, blk, slot)
            for k in range(3):
                act.wait_ge(S("sqrt_in"), k + 1)
                act.activation(sm(1), sm(0), ACT.Sqrt).then_inc(S("sqrt_out"), 1)
                if k == 1:
                    attention_act(act)
            ffn_act(act)

        @block.gpsimd
        def _(pool):
            def slot(group, turn, s, new, back_n):
                if not new:
                    return
                i, q = (group * PER_GROUP + turn) * NSTEP + s, s % QUADS
                pool.wait_ge(S("acc_high_ready"), i + 1)
                pool.tensor_tensor(acc_low[:, q, :], acc[:, q, :], acc_high[:, q, :], ALU.subtract).then_inc(S("acc_low_ready"), 1)

            for blk in range(len(GROUPS)):
                steps(pool, blk, slot)

        @block.tensor
        def _(pe):
            pe.wait_ge(S("ident_ready"), 2)

            def bank(s, n):
                return psum[:, (s % QUADS) * BANKS + n, :]

            def products(s, part, start, stop):
                for t in range(QT):
                    q = s % QUADS
                    last = pe.matmul(bank(s, t // 2)[:, (t % 2) * D:(t % 2 + 1) * D],
                                     tok_split[:, (q * QT + t) * P:(q * QT + t + 1) * P],
                                     wrow[:, s // QUADS % UNROLL, part * D:(part + 1) * D],
                                     start=(start and t % 2 == 0), stop=(stop and t % 2 == 1), skip_group_check=True)
                return last

            def add(s, eye, operand, start=False):
                for n in range(BANKS):
                    pe.matmul(bank(s, n), eye[:, :], operand[:, s % QUADS, n * 512:(n + 1) * 512],
                              start=start, stop=False, skip_group_check=True)

            def slot(group, turn, s, new, back_n):
                i = (group * PER_GROUP + turn) * NSTEP + s
                if new:
                    if s % QUADS == 0:
                        pe.wait_ge(S("row_ready"), (group * PER_GROUP + turn) * UNROLL + (s // QUADS + 1))
                    if opens(turn, s):
                        pe.wait_ge(S("quad_split"), group * QUADS + (s + 1))
                    pe.wait_ge(S("acc_ready"), i + (1 + 4 * blk))
                    products(s, 0, True, True).then_inc(S("upper_product_ready"), 1)
                if back_n(1):
                    pe.wait_ge(S("total_high_ready"), i)
                    pe.wait_ge(S("acc_high_ready"), i)
                    add(s - 1, ident_r, acc_high, start=True)
                    add(s - 1, less_ident, total_high)
                    products(s - 1, 0, False, False)
                    pe.wait_ge(S("acc_low_ready"), i)
                    add(s - 1, ident_r, acc_low)
                    products(s - 1, 1, False, True).then_inc(S("rest_ready"), 1)

            for blk in range(len(GROUPS)):
                steps(pe, blk, slot)
            for w in range(3):
                pe.wait_ge(S("w_quant"), w + 1)
                if w < 2:
                    v = wld.rearrange("p (c n) -> p c n", c=len(IC))
                    for a in range(2):
                        for c, (_, m) in enumerate(IC):
                            last = pe.transpose(psum[:, a * 2 + c // 4, (c % 4) * P:(c % 4) * P + m],
                                                v[0:m, c, a * P:(a + 1) * P], ident[0:m, 0:m])
                else:
                    v = wld[:, 0:2 * I].rearrange("p (a n) -> p a n", a=2)
                    for c, (o, m) in enumerate(IC):
                        for a in range(2):
                            last = pe.transpose(psum[0:m, c // 2, (c % 2) * D + a * P:(c % 2) * D + (a + 1) * P],
                                                v[:, a, o:o + m], ident[:, :])
                last.then_inc(S("w_turned"), 1)
            pe.wait_ge(S("energy_ready"), 1)
            pe.transpose(psum[0:B, 0, 0:T], sm(4), ident[0:T, 0:T]).then_inc(S("energy_t"), 1)
            pe.wait_ge(S("picked"), 1)
            pe.transpose(psum[0:T, 1, 0:B], tokE[:, 2, :], ident[0:B, 0:B]).then_inc(S("picked_t"), 1)
            for r in range(2):
                pe.wait_ge(S("banks_read"), r + 1)
                for n in range(8):
                    last = pe.matmul(psum[0:T, n, :], ones[0:T, :],
                                     XN.rearrange("p b n -> p (b n)")[:, (8 * r + n) * 512:(8 * r + n + 1) * 512],
                                     start=True, stop=True)
                last.then_inc(S("mean_sum"), 1)
            with pe.Fori(0, B // 2) as pairs:
                for p in range(2):
                    pe.wait_ge(S("a_rows"), pairs * 2 + (p + 1))
                    for a in range(2):
                        last = pe.transpose(psum[:, 4 * p + 3, a * T:(a + 1) * T], xb[p][:, a * P:(a + 1) * P], ident[0:T, 0:T])
                    last.then_inc(S("a_rows_turned"), 1)
                for p in range(2):
                    pe.wait_ge(S("a_rows_turned_out"), pairs * 2 + (p + 1))
                    for o in range(4):
                        for a in range(2):
                            pe.matmul(psum[:, 4 * p, o * T:(o + 1) * T], wq[:, a, o * P:(o + 1) * P], xbT[p][:, a, :],
                                      start=(a == 0), stop=(a == 1))
                    v = psum[0:T, 4 * p + 1, 0:D]
                    for a in range(2):
                        pe.matmul(v, xbT[p][:, a, :], wq[:, a, 2 * D:3 * D], start=(a == 0), stop=False)
                    pe.matmul(v, ones[0:1, :], row_bias[:, 0, :], start=False, stop=True).then_inc(S("a_qkv"), 1)
                for p in range(2):
                    pe.wait_ge(S("a_k_masked"), pairs * 2 + (p + 1))
                    for g in range(4):
                        last = pe.matmul(psum[0:T, 4 * p + g, 0:4 * T], qT[p][:, g // 2, :],
                                         kM[p][:, g // 2, (g % 2) * 4:(g % 2) * 4 + 4, :].rearrange("p h t -> p (h t)"),
                                         start=True, stop=True)
                    last.then_inc(S("a_scores"), 1)
                for p in range(2):
                    pe.wait_ge(S("a_exp"), pairs * 2 + (p + 1))
                    for h in range(HEADS):
                        last = pe.transpose(psum[0:T, 4 * p + h // 4, (h % 4) * T:(h % 4 + 1) * T], sc[p][:, h, :],
                                            ident[0:T, 0:T])
                    last.then_inc(S("a_exp_turned"), 1)
                for p in range(2):
                    pe.wait_ge(S("a_exp_turned_out"), pairs * 2 + (p + 1))
                    for h in range(HEADS):
                        last = pe.matmul(psum[0:T, 4 * p, h * HD:(h + 1) * HD], pT[p][:, h, :], vS[p][:, h * HD:(h + 1) * HD],
                                         start=True, stop=True)
                    last.then_inc(S("a_heads"), 1)
                for p in range(2):
                    pe.wait_ge(S("a_heads_scaled"), pairs * 2 + (p + 1))
                    for a in range(2):
                        last = pe.transpose(psum[:, 4 * p + 1, a * T:(a + 1) * T], cn[p][:, a * P:(a + 1) * P], ident[0:T, 0:T])
                    last.then_inc(S("a_heads_turned"), 1)
                for p in range(2):
                    pe.wait_ge(S("a_heads_turned_out"), pairs * 2 + (p + 1))
                    o = psum[0:T, 4 * p + 2, 0:D]
                    for a in range(2):
                        pe.matmul(o, cT[p][:, a, :], wo[:, a, :], start=(a == 0), stop=False)
                    pe.matmul(o, ones[0:1, :], row_bias[:, 1, :], start=False, stop=True).then_inc(S("a_projected"), 1)

            def front(b, p):
                pe.wait_ge(S("f_rows"), b + 1)
                for a in range(2):
                    last = pe.transpose(psum[:, 4 * p, a * T:(a + 1) * T], xb[p][:, a * P:(a + 1) * P], ident[0:T, 0:T])
                last.then_inc(S("f_rows_turned"), 1)
                pe.wait_ge(S("f_rows_turned_out"), b + 1)
                pe.wait_ge(S("f_down_out"), b + 1)
                for w, n in ((0, 0), (0, 1), (1, 0), (1, 1)):
                    for a in range(2):
                        last = pe.matmul(psum[0:T, 4 * p + (1 + 2 * w + n) % 4, 0:I // 2], xbT[p][:, a, :],
                                         wgu[:, w, a, n * (I // 2):(n + 1) * (I // 2)], start=(a == 0), stop=(a == 1))
                last.then_inc(S("f_gate_up"), 1)

            def back(b, p):
                pe.wait_ge(S("f_hidden_quantised"), b + 1)
                for c, (o, m) in enumerate(IC):
                    last = pe.transpose(psum[0:m, 4 * p + 1, c * T:(c + 1) * T], hid[p][:, o:o + m], ident[0:T, 0:T])
                last.then_inc(S("f_hidden_turned"), 1)
                pe.wait_ge(S("f_hidden_turned_out"), b + 1)
                for c, (_, m) in enumerate(IC):
                    last = pe.matmul(psum[0:T, 4 * p + 2, 0:D], hT[p][0:m, c, :], wd[0:m, c, :],
                                     start=(c == 0), stop=(c == len(IC) - 1))
                last.then_inc(S("f_down"), 1)

            ffn_turns(pe, front, back)

        @block.vector
        def _(dve):
            count = [0]

            def link(ins):
                count[0] += 1
                ins.then_inc(S("vec_done"), 1)
                dve.wait_ge(S("vec_done"), count[0])

            dve.sem_inc(S("raw_free"), 1)
            dve.wait_ge(S("const_dma"), 96)
            dve.tensor_copy(ident_r[:, :], ident[:, :]).then_inc(S("ident_ready"), 1)
            dve.tensor_scalar(less_ident[:, :], ident[:, :], -1.0, None, ALU.mult).then_inc(S("ident_ready"), 1)
            dve.wait_ge(S("w_dma"), 64)
            link(dve.tensor_scalar(wup.bitcast(U32), wraw.bitcast(U32), HI, None, ALU.bitwise_and))
            for j in range(KIND):
                r = slice(KG * j, KG * (j + 1))
                if j % 2 == 0:
                    dve.tensor_copy(wsplit[r], wup[r]).then_inc(S("w_split"), 1)
                else:
                    dve.tensor_tensor(wsplit[r], wraw[r], wup[r], ALU.subtract).then_inc(S("w_split"), 1)
            dve.wait_ge(S("w_split"), 4)

            def rest(s):
                b = s % QUADS * BANKS
                return psum[:, b:b + BANKS, :]

            def banks(v, s):
                return v[:, s % QUADS, :].rearrange("p (k n) -> p k n", n=512)

            def slot(group, turn, s, new, back_n):
                i = (group * PER_GROUP + turn) * NSTEP + s
                q = s % QUADS
                if back_n(2):
                    dve.wait_ge(S("rest_ready"), i - 1)
                    dve.tensor_tensor(banks(acc, s - 2), rest(s - 2), banks(total_high, s - 2),
                                      ALU.add).then_inc(S("acc_ready"), 1)
                if new:
                    dve.wait_ge(S("upper_product_ready"), i + 1)
                    dve.wait_ge(S("acc_ready"), i + (1 + 4 * blk))
                    dve.tensor_tensor(banks(total_high, s), rest(s), banks(acc, s), ALU.add).then_inc(S("total_high_ready"), 1)

            def split(group):
                dve.wait_ge(S("raw_dma"), (group + 1) * 64)
                dve.tensor_scalar(halves.bitcast(U32), raw.bitcast(U32), HI, None,
                                  ALU.bitwise_and).then_inc(S("split_hi"), 1)
                dve.wait_ge(S("split_hi"), group + 1)
                dve.tensor_tensor(halves[2 * KG:P, :], raw[2 * KG:P, :], halves[2 * KG:P, :],
                                  ALU.subtract).then_inc(S("split_dve"), 1)
                dve.wait_ge(S("split_dve"), group + 1)
                dve.sem_inc(S("raw_free"), 1)

            def split_next(group):
                dve.wait_ge(S("quad_split"), (group + 1) * QUADS)
                split(group + 1)

            split(0)
            for blk in range(len(GROUPS)):
                dve.memset(acc, 0.0).then_inc(S("acc_ready"), 4)
                steps(dve, blk, slot, split_next)
                done = sum(GROUPS[:blk + 1]) * PER_GROUP * NSTEP + 4 * (blk + 1)
                dve.wait_ge(S("acc_ready"), done)
                if blk == 0:
                    link(dve.tensor_copy(first, acc))
                else:
                    dve.tensor_tensor(acc, first, acc, ALU.add).then_inc(S("tokens_done"), 1)

            def fp4(x, a, c, top, scale):
                n = x.free_size() // FB
                blocks = lambda v: v.rearrange("p (b s) -> p b s", s=FB)
                wide = lambda v: v.unsqueeze(2).to_broadcast([v.shape[0], n, FB])

                def above(k):
                    return dve.scalar_tensor_tensor(out=c, in0=a, scalar=MIDS[k], in1=c, op0=ALU.is_gt, op1=ALU.add)
                link(dve.tensor_reduce(top, blocks(x), X, ALU.max, apply_absolute_value=True))
                link(dve.tensor_scalar(top, top, 1.0 / 6.0, 1e-12, ALU.mult, ALU.max))
                link(dve.reciprocal(scale, top))
                link(dve.tensor_scalar(a.bitcast(U32), x.bitcast(U32), 0x7FFFFFFF, None, ALU.bitwise_and))
                link(dve.tensor_tensor(blocks(a), blocks(a), wide(scale), ALU.mult))
                dve.tensor_scalar(top, top, 0.5, None, ALU.mult)
                link(dve.tensor_scalar(c, a, MIDS[6], 2.0, ALU.is_gt, ALU.mult))
                link(above(5))
                link(above(4))
                link(dve.tensor_scalar(c, c, 2.0, None, ALU.mult))
                for k in range(4):
                    link(above(k))
                link(dve.tensor_tensor(blocks(c), blocks(c), wide(top), ALU.mult))
                return dve.scalar_tensor_tensor(out=x.bitcast(U32), in0=x.bitcast(U32), scalar=0x80000000,
                                                in1=c.bitcast(U32), op0=ALU.bitwise_and, op1=ALU.bitwise_or)

            dve.wait_ge(S("tokens_done"), 1)
            dve.wait_ge(S("h_dma"), 80)
            dve.memset(ones[:, :], 1.0)
            link(dve.memset(wld, 0.0))
            dve.sem_inc(S("wld_free"), 1)
            for w in range(3):
                dve.wait_ge(S("wld_dma"), 32 * (w + 1))
                n = 6 * D if w < 2 else 2 * I
                fp4(wld[:, 0:n], wa[:, 0:n], wc[:, 0:n],
                    wmax[:, 0, 0:n // FB], wmax[:, 1, 0:n // FB]).then_inc(S("w_quant"), 1)
                dve.wait_ge(S("w_turned"), w + 1)
                if w < 2:
                    for a in range(2):
                        dve.tensor_copy(wgu[:, w, a, 0:512], psum[:, a * 2, :])
                        last = dve.tensor_copy(wgu[:, w, a, 512:I], psum[:, a * 2 + 1, 0:I - 512])
                else:
                    for c, (_, m) in enumerate(IC):
                        last = dve.tensor_copy(wd[0:m, c, :], psum[0:m, c // 2, (c % 2) * D:(c % 2 + 1) * D])
                link(last)
                dve.sem_inc(S("wld_free"), 1)

            def wide(v, n=D):
                return v.unsqueeze(2).to_broadcast([T, v.shape[1], n])

            def root(k, n):
                y, yh, yl, r, t = sm(1), sm(13), sm(14), sm(15), sm(16)
                dve.sem_inc(S("sqrt_in"), 1)
                dve.wait_ge(S("sqrt_out"), n)
                link(dve.tensor_scalar(yh.bitcast(U32), y.bitcast(U32), HI, None, ALU.bitwise_and))
                link(dve.tensor_tensor(yl, y, yh, ALU.subtract))
                link(dve.tensor_tensor(t, yh, yh, ALU.mult))
                link(dve.tensor_tensor(r, sm(0), t, ALU.subtract))
                link(dve.scalar_tensor_tensor(out=t, in0=yh, scalar=2.0, in1=yl, op0=ALU.mult, op1=ALU.mult))
                link(dve.tensor_tensor(r, r, t, ALU.subtract))
                link(dve.tensor_tensor(t, yl, yl, ALU.mult))
                link(dve.tensor_tensor(r, r, t, ALU.subtract))
                link(dve.tensor_scalar(t, y, 2.0, 1e-30, ALU.mult, ALU.max))
                link(dve.reciprocal(t, t))
                link(dve.tensor_tensor(r, r, t, ALU.mult))
                link(dve.tensor_tensor(sm(k), y, r, ALU.add))

            def mean_lanes(src, k):
                ln = lanes[0:T, :].rearrange("p (b l) -> p b l", l=16)
                link(dve.tensor_reduce(ln, src.rearrange("p b (i l) -> p b l i", l=16), X, ALU.add))
                link(dve.tensor_tensor(ln[:, :, 0:4], ln[:, :, 0:4], ln[:, :, 4:8], ALU.add))
                link(dve.tensor_tensor(ln[:, :, 8:12], ln[:, :, 8:12], ln[:, :, 12:16], ALU.add))
                link(dve.tensor_tensor(ln[:, :, 0:4], ln[:, :, 0:4], ln[:, :, 8:12], ALU.add))
                link(dve.tensor_tensor(ln[:, :, 0:4:2], ln[:, :, 0:4:2], ln[:, :, 1:4:2], ALU.add))
                link(dve.tensor_tensor(ln[:, :, 0:1], ln[:, :, 0:1], ln[:, :, 2:3], ALU.add))
                link(dve.tensor_scalar(sm(k), ln[:, :, 0], 1.0 / D, None, ALU.mult))

            def squares(src, k):
                link(dve.tensor_tensor(T1, src, src, ALU.mult))
                w8 = lanes[0:T, 0:8 * B].rearrange("p (b w) -> p b w", w=8)
                link(dve.tensor_reduce(w8, T1.rearrange("p b (w s) -> p b w s", s=32), X, ALU.add))
                link(dve.tensor_reduce(sm(k), w8, X, ALU.add))

            def deviation(n):
                mean_lanes(H, 2)
                link(dve.tensor_tensor(XN, H, wide(sm(2)), ALU.subtract))
                squares(XN, 3)
                link(dve.tensor_scalar(sm(0), sm(3), 1.0 / D, EPS, ALU.mult, ALU.add))
                root(5, n)

            deviation(1)
            sh, sl, rs = sm(6), sm(7), sm(8)
            link(dve.tensor_scalar(sh.bitcast(U32), sm(5).bitcast(U32), HI, None, ALU.bitwise_and))
            link(dve.tensor_tensor(sl, sm(5), sh, ALU.subtract))
            link(dve.reciprocal(rs, sm(5)))
            for c in range(4):
                i = slice(8 * c, 8 * c + 8)
                d = XN[:, i, :]
                q0, qh, ql, pr = T1[:, 0:8, :], T1[:, 8:16, :], T1[:, 16:24, :], T1[:, 24:32, :]
                wsh, wsl, wrs = (wide(v[:, i]) for v in (sh, sl, rs))
                rem = T2[:, 0:8, :]
                link(dve.tensor_tensor(q0, d, wrs, ALU.mult))
                link(dve.tensor_scalar(qh.bitcast(U32), q0.bitcast(U32), HI, None, ALU.bitwise_and))
                link(dve.tensor_tensor(ql, q0, qh, ALU.subtract))
                link(dve.tensor_tensor(pr, qh, wsh, ALU.mult))
                link(dve.tensor_tensor(rem, d, pr, ALU.subtract))
                for qx, sx in ((qh, wsl), (ql, wsh), (ql, wsl)):
                    link(dve.tensor_tensor(pr, qx, sx, ALU.mult))
                    link(dve.tensor_tensor(rem, rem, pr, ALU.subtract))
                link(dve.tensor_tensor(rem, rem, wrs, ALU.mult))
                link(dve.tensor_tensor(d, q0, rem, ALU.add))
            squares(XN, 0)
            root(4, 2)
            dve.sem_inc(S("energy_ready"), 1)
            dve.sem_inc(S("lanes_free"), 1)

            dve.wait_ge(S("energy_t"), 1)
            link(dve.tensor_copy(tokE[:, 0, :], psum[0:B, 0, 0:T]))
            ej = tokE[:, 0, :].unsqueeze(1).to_broadcast([B, T, T])
            ei = tokE[:, 0, :].unsqueeze(2).to_broadcast([B, T, T])
            dve.wait_ge(S("earl_dma"), 16)
            dve.tensor_tensor(gt, ej, ei, ALU.is_gt)
            link(dve.tensor_tensor(eq, ej, ei, ALU.is_equal))
            link(dve.tensor_tensor(eq, eq, earl, ALU.mult))
            link(dve.tensor_tensor(gt, gt, eq, ALU.add))
            link(dve.tensor_reduce(tokE[:, 1, :], gt, X, ALU.add))
            dve.tensor_scalar(tokE[:, 2, :], tokE[:, 1, :], float(TOPK), None, ALU.is_lt).then_inc(S("picked"), 1)
            dve.wait_ge(S("picked_t"), 1)
            link(dve.tensor_copy(sm(9), psum[0:T, 1, 0:B]))
            dve.sem_inc(S("banks_read"), 1)
            link(dve.tensor_scalar(sm(10), sm(9), -1.0 / T, 1.0 / T, ALU.mult, ALU.add))
            for r in range(2):
                dve.wait_ge(S("mean_sum"), r + 1)
                i = slice(16 * r, 16 * r + 16)
                ps = psum[0:T, :, :].rearrange("p k (b n) -> p (k b) n", n=D)
                ins = dve.tensor_tensor(T1[:, i, :], ps, wide(sm(10)[:, i]), ALU.mult)
                link(ins)
                dve.sem_inc(S("banks_read"), 1)
            link(dve.tensor_tensor(H, H, T1, ALU.add))
            for p in range(2):
                dve.sem_inc(S(f"a_buffers_free{p}"), 1)

            with dve.Fori(0, B // 2) as pairs:
                for p in range(2):
                    dve.wait_ge(S("a_rows_turned"), pairs * 2 + (p + 1))
                    dve.tensor_copy(xbT[p].rearrange("p a t -> p (a t)"), psum[:, 4 * p + 3, 0:2 * T]).then_inc(S("a_rows_turned_out"), 1)
                for p in range(2):
                    dve.wait_ge(S("a_qkv_out"), pairs * 2 + (p + 1))
                    for o in range(2):
                        ins = dve.tensor_tensor(kM[p][:, o, :, :], kT[p][:, o, :].unsqueeze(1).to_broadcast([P, 8, T]),
                                                hmask[:, :].unsqueeze(2).to_broadcast([P, 8, T]), ALU.mult)
                    ins.then_inc(S("a_k_masked"), 1)
                for p in range(2):
                    s4 = psum[0:T, 4 * p:4 * p + 4, 0:4 * T].rearrange("p g (h t) -> p g h t", t=T)
                    dve.wait_ge(S("a_scores"), pairs * 2 + (p + 1))
                    dve.tensor_reduce(mx[p].rearrange("p (g h) -> p g h", g=4), s4, X, ALU.max).then_inc(S("a_max"), 1)
                    dve.wait_ge(S("a_max"), pairs * 2 + (p + 1))
                    for g in range(4):
                        ins = dve.tensor_tensor(sc[p][:, 4 * g:4 * g + 4, :], s4[:, g, :, :],
                                                mx[p][:, 4 * g:4 * g + 4].unsqueeze(2).to_broadcast([T, 4, T]), ALU.subtract)
                    ins.then_inc(S("a_scores_less_max"), 1)
                for p in range(2):
                    dve.wait_ge(S("a_exp"), pairs * 2 + (p + 1))
                    dve.tensor_reduce(den[p], sc[p], X, ALU.add).then_inc(S("a_exp_sums"), 1)
                for p in range(2):
                    dve.wait_ge(S("a_exp_sums"), pairs * 2 + (p + 1))
                    dve.reciprocal(rden[p], den[p]).then_inc(S("a_exp_sums_inverse"), 1)
                for p in range(2):
                    heads = lambda v: v.rearrange("p (h e) -> p h e", e=HD)
                    dve.wait_ge(S("a_heads"), pairs * 2 + (p + 1))
                    dve.wait_ge(S("a_exp_sums_inverse"), pairs * 2 + (p + 1))
                    dve.tensor_tensor(heads(cn[p]), heads(psum[0:T, 4 * p, 0:D]),
                                      rden[p].unsqueeze(2).to_broadcast([T, HEADS, HD]), ALU.mult).then_inc(S("a_heads_scaled"), 1)
                for p in range(2):
                    dve.wait_ge(S("a_heads_turned"), pairs * 2 + (p + 1))
                    dve.tensor_copy(cT[p].rearrange("p a t -> p (a t)"), psum[:, 4 * p + 1, 0:2 * T]).then_inc(S("a_heads_turned_out"), 1)
                for p in range(2):
                    b = pairs * 2 + p
                    dve.wait_ge(S("a_projected"), pairs * 2 + (p + 1))
                    hb = H[:, bass.ds(b, 1), :].rearrange("p a n -> p (a n)")
                    dve.scalar_tensor_tensor(out=hb, in0=psum[0:T, 4 * p + 2, 0:D], scalar=small[0:T, 9, bass.ds(b, 1)],
                                             in1=hb, op0=ALU.mult, op1=ALU.add).then_inc(S(f"a_buffers_free{p}"), 1)
            for p in range(2):
                dve.wait_ge(S(f"a_buffers_free{p}"), B // 2 + 1)

            deviation(3)
            link(dve.reciprocal(sm(8), sm(5)))
            link(dve.tensor_tensor(XN, XN, wide(sm(8)), ALU.mult))
            xf = XN.rearrange("p b n -> p (b n)")
            t1, t2 = T1.rearrange("p b n -> p (b n)"), T2.rearrange("p b n -> p (b n)")
            for c in range(4):
                n = W8 // 4
                link(fp4(xf[:, c * n:(c + 1) * n], t1[:, 0:n], t1[:, n:2 * n],
                         t2[:, 0:n // FB], t2[:, n // FB:2 * n // FB]))
            dve.sem_inc(S("f_down_out"), 2)
            dve.sem_inc(S("ffn_rows"), 1)
            N_LINKS = 15

            def front(b, p):
                nonlocal link
                per = [0]

                def link(ins):
                    per[0] += 1
                    ins.then_inc(S("vec_image_done"), 1)
                    dve.wait_ge(S("vec_image_done"), b * N_LINKS + per[0])

                dve.wait_ge(S("f_silu"), b + 1)
                for n in range(2):
                    part = slice(n * (I // 2), (n + 1) * (I // 2))
                    ins = dve.tensor_tensor(hid[p][:, part], psum[0:T, 4 * p + (3 + n) % 4, 0:I // 2], gate[p][:, part], ALU.mult)
                link(ins)
                fp4(hid[p], qa[p], qc[p], bmax[p][:, 0, :], bmax[p][:, 1, :]).then_inc(S("f_hidden_quantised"), 1)
                assert per[0] == N_LINKS, per[0]

            def back(b, p):
                hb = H[:, bass.ds(b, 1), :].rearrange("p a n -> p (a n)")
                dve.wait_ge(S("f_down_out"), b + 3)
                dve.tensor_tensor(hb, ffn_out[p], hb, ALU.add).then_inc(S("f_added"), 1)

            ffn_turns(dve, front, back)

    return nc


def kernel(x, cls_tok, L0_tok_W, L0_attn_in_proj_w, L0_attn_in_proj_b, L0_attn_out_w, L0_attn_out_b,
           L0_ffn_w_gate, L0_ffn_w_up, L0_ffn_w_down):
    import numpy as np
    import concourse.bacc as bacc
    from concourse.bass_utils import run_bass_kernel_spmd as run

    s = 16
    x = np.asarray(x)
    xT = x.reshape(B, 8, s, 8, s, 3).transpose(2, 4, 5, 0, 1, 3).reshape(F, B * NP_TOK)
    p = np.arange(P)
    kind0 = (p[:, None] < KG) & (p[:, None] % KG == np.arange(KG)[None])
    kinds = (p[:, None] >= KG) & (p[:, None] % KG == np.arange(KG)[None])
    masks = np.stack([kind0, kinds], 1).astype(np.float32)
    place = np.concatenate([np.arange(1, T), [0]])
    earlier = np.broadcast_to((place[None, :] < place[:, None]), (B, T, T)).astype(np.float32)
    head = (p[:, None] // HD == np.arange(8)[None]).astype(np.float32)
    arrays = {
        "xT": xT, "cls_tok": cls_tok, "w_tok": L0_tok_W, "in_wT": np.asarray(L0_attn_in_proj_w).T,
        "in_b": L0_attn_in_proj_b, "in_bT": np.asarray(L0_attn_in_proj_b).reshape(6, P).T, "out_wT": np.asarray(L0_attn_out_w).T, "out_b": L0_attn_out_b,
        "w_gate": L0_ffn_w_gate, "w_up": L0_ffn_w_up, "w_down": L0_ffn_w_down,
        "feature_masks": masks, "earlier": earlier, "head_mask": head, "identity": np.eye(P, dtype=np.float32),
    }
    arrays = {n + "_in": np.ascontiguousarray(a) for n, a in arrays.items()}
    nc = bacc.Bacc("TRN2", target_bir_lowering=False, num_devices=1)
    args = [nc.dram_tensor(n, a.shape, mybir.dt.from_np(a.dtype), kind="ExternalInput").ap() for n, a in arrays.items()]
    o = nc.dram_tensor("out_0", (B, T, D), F32, kind="ExternalOutput").ap()
    build_vit(nc, *args, o)
    return run(nc, [arrays], core_ids=[0]).results[0]["out_0"]
```
